# Optimizing a Trainium2 kernel written in Bass

```python
import numpy as np
import jax
import jax.numpy as jnp

def _softmax(x, axis=-1):
    return jax.nn.softmax(x, axis=axis)

def _gelu(x):
    return jax.nn.gelu(x, approximate=True)

def _silu(x):
    return jax.nn.silu(x)

def _sigmoid(x):
    return jax.nn.sigmoid(x)

def _layernorm(x, axis=-1, eps=1e-05):
    m = jnp.mean(x, axis=axis, keepdims=True)
    v = jnp.var(x, axis=axis, keepdims=True)
    return (x - m) / jnp.sqrt(v + eps)

def _scatter_add(tgt, idx, src, axis=0):
    return tgt.at[idx].add(src)

def _segment_sum(src, seg, n):
    return jax.ops.segment_sum(src, seg, n)
kernel_name = 'mk_dlrm_tower_d1_rec_r8_c971e3'

def setup_inputs(seed: int=0):
    np.random.seed(seed)
    _w = jnp.asarray

    def _rec_inputs():
        import jax
        import jax.numpy as jnp
        _tk = jax.random.key(seed)
        dense_ctx = jax.random.normal(jax.random.fold_in(_tk, 190), (512, 16), jnp.float32)
        ids = jnp.stack([jax.random.randint(jax.random.fold_in(_tk, 200 + f), (512,), 0, v, jnp.int32) for f, v in enumerate([12500, 1000, 1000, 12500, 125000, 125000, 125000, 12500, 1250, 12500, 12500, 125000, 125000, 1250, 12500, 125000, 12500, 1250, 1250, 125000, 1250, 1250, 1000, 1250, 1250, 1250, 1250, 1000, 1000, 1000, 1000, 1000])], axis=1)
        tbl_0 = 0.05 * jax.random.normal(jax.random.fold_in(_tk, 500 + 0), (12500, 32), jnp.float32)
        tbl_1 = 0.05 * jax.random.normal(jax.random.fold_in(_tk, 500 + 1), (1000, 32), jnp.float32)
        tbl_2 = 0.05 * jax.random.normal(jax.random.fold_in(_tk, 500 + 2), (1000, 32), jnp.float32)
        tbl_3 = 0.05 * jax.random.normal(jax.random.fold_in(_tk, 500 + 3), (12500, 32), jnp.float32)
        tbl_4 = 0.05 * jax.random.normal(jax.random.fold_in(_tk, 500 + 4), (125000, 32), jnp.float32)
        tbl_5 = 0.05 * jax.random.normal(jax.random.fold_in(_tk, 500 + 5), (125000, 32), jnp.float32)
        tbl_6 = 0.05 * jax.random.normal(jax.random.fold_in(_tk, 500 + 6), (125000, 32), jnp.float32)
        tbl_7 = 0.05 * jax.random.normal(jax.random.fold_in(_tk, 500 + 7), (12500, 32), jnp.float32)
        tbl_8 = 0.05 * jax.random.normal(jax.random.fold_in(_tk, 500 + 8), (1250, 32), jnp.float32)
        tbl_9 = 0.05 * jax.random.normal(jax.random.fold_in(_tk, 500 + 9), (12500, 32), jnp.float32)
        tbl_10 = 0.05 * jax.random.normal(jax.random.fold_in(_tk, 500 + 10), (12500, 32), jnp.float32)
        tbl_11 = 0.05 * jax.random.normal(jax.random.fold_in(_tk, 500 + 11), (125000, 32), jnp.float32)
        tbl_12 = 0.05 * jax.random.normal(jax.random.fold_in(_tk, 500 + 12), (125000, 32), jnp.float32)
        tbl_13 = 0.05 * jax.random.normal(jax.random.fold_in(_tk, 500 + 13), (1250, 32), jnp.float32)
        tbl_14 = 0.05 * jax.random.normal(jax.random.fold_in(_tk, 500 + 14), (12500, 32), jnp.float32)
        tbl_15 = 0.05 * jax.random.normal(jax.random.fold_in(_tk, 500 + 15), (125000, 32), jnp.float32)
        tbl_16 = 0.05 * jax.random.normal(jax.random.fold_in(_tk, 500 + 16), (12500, 32), jnp.float32)
        tbl_17 = 0.05 * jax.random.normal(jax.random.fold_in(_tk, 500 + 17), (1250, 32), jnp.float32)
        tbl_18 = 0.05 * jax.random.normal(jax.random.fold_in(_tk, 500 + 18), (1250, 32), jnp.float32)
        tbl_19 = 0.05 * jax.random.normal(jax.random.fold_in(_tk, 500 + 19), (125000, 32), jnp.float32)
        tbl_20 = 0.05 * jax.random.normal(jax.random.fold_in(_tk, 500 + 20), (1250, 32), jnp.float32)
        tbl_21 = 0.05 * jax.random.normal(jax.random.fold_in(_tk, 500 + 21), (1250, 32), jnp.float32)
        tbl_22 = 0.05 * jax.random.normal(jax.random.fold_in(_tk, 500 + 22), (1000, 32), jnp.float32)
        tbl_23 = 0.05 * jax.random.normal(jax.random.fold_in(_tk, 500 + 23), (1250, 32), jnp.float32)
        tbl_24 = 0.05 * jax.random.normal(jax.random.fold_in(_tk, 500 + 24), (1250, 32), jnp.float32)
        tbl_25 = 0.05 * jax.random.normal(jax.random.fold_in(_tk, 500 + 25), (1250, 32), jnp.float32)
        tbl_26 = 0.05 * jax.random.normal(jax.random.fold_in(_tk, 500 + 26), (1250, 32), jnp.float32)
        tbl_27 = 0.05 * jax.random.normal(jax.random.fold_in(_tk, 500 + 27), (1000, 32), jnp.float32)
        tbl_28 = 0.05 * jax.random.normal(jax.random.fold_in(_tk, 500 + 28), (1000, 32), jnp.float32)
        tbl_29 = 0.05 * jax.random.normal(jax.random.fold_in(_tk, 500 + 29), (1000, 32), jnp.float32)
        tbl_30 = 0.05 * jax.random.normal(jax.random.fold_in(_tk, 500 + 30), (1000, 32), jnp.float32)
        tbl_31 = 0.05 * jax.random.normal(jax.random.fold_in(_tk, 500 + 31), (1000, 32), jnp.float32)
        _rk = jax.random.fold_in(_tk, 7)
        W_top1 = 0.0606339 * jax.random.normal(jax.random.fold_in(_tk, 801), (272, 512), jnp.float32)
        W_top2 = 0.0441942 * jax.random.normal(jax.random.fold_in(_tk, 802), (512, 256), jnp.float32)
        W_top3 = 0.0625 * jax.random.normal(jax.random.fold_in(_tk, 803), (256, 1), jnp.float32)
        b_top1 = jnp.zeros((512,), jnp.float32)
        b_top2 = jnp.zeros((256,), jnp.float32)
        return (dense_ctx, ids, tbl_0, tbl_1, tbl_2, tbl_3, tbl_4, tbl_5, tbl_6, tbl_7, tbl_8, tbl_9, tbl_10, tbl_11, tbl_12, tbl_13, tbl_14, tbl_15, tbl_16, tbl_17, tbl_18, tbl_19, tbl_20, tbl_21, tbl_22, tbl_23, tbl_24, tbl_25, tbl_26, tbl_27, tbl_28, tbl_29, tbl_30, tbl_31, W_top1, b_top1, W_top2, b_top2, W_top3)
    dense_ctx, ids, tbl_0, tbl_1, tbl_2, tbl_3, tbl_4, tbl_5, tbl_6, tbl_7, tbl_8, tbl_9, tbl_10, tbl_11, tbl_12, tbl_13, tbl_14, tbl_15, tbl_16, tbl_17, tbl_18, tbl_19, tbl_20, tbl_21, tbl_22, tbl_23, tbl_24, tbl_25, tbl_26, tbl_27, tbl_28, tbl_29, tbl_30, tbl_31, W_top1, b_top1, W_top2, b_top2, W_top3 = _rec_inputs()

    def _L0_rec_setup():
        import jax, jax.numpy as jnp
        import numpy as np
        B, F, D = (512, 32, 32)
        LAYER_SIZE = [128, 128]

        def _cin_forward(inputs, filters):
            x0 = inputs
            prev = inputs
            outs = []
            for W in filters:
                z = jnp.einsum('bhd,bmd->bhmd', x0, prev)
                b, h, m, d = z.shape
                z = z.reshape(b, h * m, d)
                cur = jnp.einsum('bpd,pn->bnd', z, W[0])
                cur = jax.nn.relu(cur)
                prev = cur
                outs.append(cur)
            result = jnp.concatenate(outs, axis=1)
            return jnp.sum(result, axis=-1)
        key = jax.random.key(seed)
        k1, k2, k3 = jax.random.split(key, 3)
        inputs = jax.random.normal(k1, (B, F, D), dtype=jnp.float32)
        field_nums = [F] + LAYER_SIZE
        filter_0 = jax.random.normal(k2, (1, field_nums[0] * field_nums[0], field_nums[1]), dtype=jnp.float32) * 0.05
        filter_1 = jax.random.normal(k3, (1, field_nums[0] * field_nums[1], field_nums[2]), dtype=jnp.float32) * 0.05
        return {'inputs': inputs, 'filter_0': filter_0, 'filter_1': filter_1}
    _L0_rec_all = _L0_rec_setup()
    _L0_rec_in = {k: v for k, v in _L0_rec_all.items() if k in ('filter_0', 'filter_1')}
    del _L0_rec_all
    return {'dense_ctx': dense_ctx, 'ids': ids, 'tbl_0': tbl_0, 'tbl_1': tbl_1, 'tbl_2': tbl_2, 'tbl_3': tbl_3, 'tbl_4': tbl_4, 'tbl_5': tbl_5, 'tbl_6': tbl_6, 'tbl_7': tbl_7, 'tbl_8': tbl_8, 'tbl_9': tbl_9, 'tbl_10': tbl_10, 'tbl_11': tbl_11, 'tbl_12': tbl_12, 'tbl_13': tbl_13, 'tbl_14': tbl_14, 'tbl_15': tbl_15, 'tbl_16': tbl_16, 'tbl_17': tbl_17, 'tbl_18': tbl_18, 'tbl_19': tbl_19, 'tbl_20': tbl_20, 'tbl_21': tbl_21, 'tbl_22': tbl_22, 'tbl_23': tbl_23, 'tbl_24': tbl_24, 'tbl_25': tbl_25, 'tbl_26': tbl_26, 'tbl_27': tbl_27, 'tbl_28': tbl_28, 'tbl_29': tbl_29, 'tbl_30': tbl_30, 'tbl_31': tbl_31, 'W_top1': W_top1, 'b_top1': b_top1, 'W_top2': W_top2, 'b_top2': b_top2, 'W_top3': W_top3, 'L0_rec_filter_0': _L0_rec_in['filter_0'], 'L0_rec_filter_1': _L0_rec_in['filter_1']}

def reference(dense_ctx, ids, tbl_0, tbl_1, tbl_2, tbl_3, tbl_4, tbl_5, tbl_6, tbl_7, tbl_8, tbl_9, tbl_10, tbl_11, tbl_12, tbl_13, tbl_14, tbl_15, tbl_16, tbl_17, tbl_18, tbl_19, tbl_20, tbl_21, tbl_22, tbl_23, tbl_24, tbl_25, tbl_26, tbl_27, tbl_28, tbl_29, tbl_30, tbl_31, W_top1, b_top1, W_top2, b_top2, W_top3, L0_rec_filter_0, L0_rec_filter_1):
    import jax
    import jax.numpy as jnp

    def _L0_rec_ref(inputs, filter_0, filter_1):
        import jax, jax.numpy as jnp
        import numpy as np
        B, F, D = (512, 32, 32)
        LAYER_SIZE = [128, 128]

        def _cin_forward(inputs, filters):
            x0 = inputs
            prev = inputs
            outs = []
            for W in filters:
                z = jnp.einsum('bhd,bmd->bhmd', x0, prev)
                b, h, m, d = z.shape
                z = z.reshape(b, h * m, d)
                cur = jnp.einsum('bpd,pn->bnd', z, W[0])
                cur = jax.nn.relu(cur)
                prev = cur
                outs.append(cur)
            result = jnp.concatenate(outs, axis=1)
            return jnp.sum(result, axis=-1)
        return _cin_forward(inputs, (filter_0, filter_1))
    e = jnp.stack([tbl_0[ids[:, 0]], tbl_1[ids[:, 1]], tbl_2[ids[:, 2]], tbl_3[ids[:, 3]], tbl_4[ids[:, 4]], tbl_5[ids[:, 5]], tbl_6[ids[:, 6]], tbl_7[ids[:, 7]], tbl_8[ids[:, 8]], tbl_9[ids[:, 9]], tbl_10[ids[:, 10]], tbl_11[ids[:, 11]], tbl_12[ids[:, 12]], tbl_13[ids[:, 13]], tbl_14[ids[:, 14]], tbl_15[ids[:, 15]], tbl_16[ids[:, 16]], tbl_17[ids[:, 17]], tbl_18[ids[:, 18]], tbl_19[ids[:, 19]], tbl_20[ids[:, 20]], tbl_21[ids[:, 21]], tbl_22[ids[:, 22]], tbl_23[ids[:, 23]], tbl_24[ids[:, 24]], tbl_25[ids[:, 25]], tbl_26[ids[:, 26]], tbl_27[ids[:, 27]], tbl_28[ids[:, 28]], tbl_29[ids[:, 29]], tbl_30[ids[:, 30]], tbl_31[ids[:, 31]]], axis=1)
    z = _L0_rec_ref(e, L0_rec_filter_0, L0_rec_filter_1)
    z = z.reshape(z.shape[0], -1)
    h = jnp.concatenate([z, dense_ctx], axis=1)
    h = jnp.maximum(h @ W_top1 + b_top1, 0.0)
    h = jnp.maximum(h @ W_top2 + b_top2, 0.0)
    y = h @ W_top3
    return y

_drawn_inputs = setup_inputs


def setup_inputs(seed=0):
    import zlib

    import numpy as np

    out = dict(_drawn_inputs(seed))
    spreads = {'b_top1': (0.0, 0.445), 'b_top2': (0.0, 0.437)}
    factors = {'tbl_0': 6.132,
     'tbl_1': 6.308,
     'tbl_2': 5.912,
     'tbl_3': 6.229,
     'tbl_4': 6.08,
     'tbl_5': 6.271,
     'tbl_6': 6.047,
     'tbl_7': 6.535,
     'tbl_8': 6.326,
     'tbl_9': 6.358,
     'tbl_10': 5.761,
     'tbl_11': 5.741,
     'tbl_12': 5.93,
     'tbl_13': 6.235,
     'tbl_14': 6.155,
     'tbl_15': 5.934,
     'tbl_16': 6.493,
     'tbl_17': 5.96,
     'tbl_18': 6.221,
     'tbl_19': 6.171,
     'tbl_20': 6.118,
     'tbl_21': 6.441,
     'tbl_22': 6.325,
     'tbl_23': 6.15,
     'tbl_24': 6.643,
     'tbl_25': 5.828,
     'tbl_26': 5.627,
     'tbl_27': 6.107,
     'tbl_28': 6.39,
     'tbl_29': 6.087,
     'tbl_30': 6.054,
     'tbl_31': 5.908,
     'L0_rec_filter_1': 8.0}
    for name, (base, spread) in spreads.items():
        noise = np.random.default_rng([zlib.crc32(name.encode()), seed]).standard_normal(out[name].shape)
        drawn = base * np.exp(spread * noise) if base else spread * noise
        out[name] = jnp.asarray(drawn.astype(out[name].dtype))
    for name, factor in factors.items():
        out[name] = (out[name] * factor).astype(out[name].dtype)
    return out
```

```python
from contextlib import ExitStack

import concourse.bass as bass
from concourse import mybir

F32 = mybir.dt.float32
I32 = mybir.dt.int32
U32 = mybir.dt.uint32
ALU = mybir.AluOpType
ACT = mybir.ActivationFunctionType
AX = mybir.AxisListType

P = 128
FIELDS = 32
DIM = 32
MAPS = 128
GROUPS = 4
PER_GROUP = DIM // GROUPS
HALF = PER_GROUP // 2
COLS = HALF * P
HQ, HI = 8, 4
MQ, MJ = 16, 8
SHIFTS = 16
ST = 4
RING = 4
DMA = 16


def build_cin_tower(nc: bass.Bass, dense_t, ids, tables, w_top1, b_top1, w_top2, b_top2, w_top3,
                    w0_wide, w0_tall, w1, identity, out):
    B = ids.shape[0]
    TILES = B // P
    STRIPS = TILES * 2 * GROUPS
    CTX = dense_t.shape[0]
    N1, N2 = w_top1.shape[1], w_top2.shape[1]
    M1, M2 = N1 // P, N2 // P

    x_rows = nc.dram_tensor("x_rows", [STRIPS, 2 * FIELDS, COLS], F32).ap()
    cur0_rows = nc.dram_tensor("cur0_rows", [2, MAPS, COLS], F32).ap()

    with ExitStack() as ctx:
        def sb(name, shape, dt=F32):
            return ctx.enter_context(nc.sbuf_tensor(name, shape, dt))

        def psum(name, shape):
            return ctx.enter_context(nc.psum_tensor(name, shape, F32))

        def sem(name):
            return ctx.enter_context(nc.semaphore(name))

        ids_sb = sb("ids_sb", [P, TILES, FIELDS], I32)
        emb = sb("emb", [P, TILES, FIELDS, DIM])
        ident = sb("ident", [P, P])
        xt = sb("xt", [P, 2, COLS])
        w0 = sb("w0", [P, ST, MAPS])
        w0_last = sb("w0_last", [SHIFTS, MAPS])
        w1_sb = sb("w1_sb", [P, HI, MJ, MAPS])
        x_shift = sb("x_shift", [P, 2, ST, COLS])
        x_four = sb("x_four", [P, 2, COLS])
        x_far = sb("x_far", [SHIFTS, 2, COLS])
        x_rep = sb("x_rep", [P, 2, HI, COLS])
        cur0 = sb("cur0", [P, 2, COLS])
        cur0_rep = sb("cur0_rep", [P, 2, MJ, COLS])
        z0 = sb("z0", [P, ST, COLS])
        z0_last = sb("z0_last", [SHIFTS, COLS])
        z1 = sb("z1", [P, RING, HI, COLS])
        acc = sb("acc", [P, 2, TILES, COLS])
        pooled = sb("pooled", [P, 2, B])
        ctx_sb = sb("ctx_sb", [CTX, B])
        wt1 = sb("wt1", [P, 2, N1])
        wt1_ctx = sb("wt1_ctx", [CTX, N1])
        wt2 = sb("wt2", [P, M1, N2])
        wt3 = sb("wt3", [P, M2])
        bt1 = sb("bt1", [P, M1])
        bt2 = sb("bt2", [P, M2])
        w0a, w0b = z1[:, 0, :, 0:MAPS], z1[:, 1, :, 0:MAPS]
        w0a_last, w0b_last = z1[0:SHIFTS, 2, 0, 0:MAPS], z1[0:SHIFTS, 2, 1, 0:MAPS]
        h1, h2, y_sb = z1[:, 0, 0:M1, 0:B], z1[:, 1, 0:M2, 0:B], z1[0:1, 2, 0, 0:B]

        ps_x = psum("ps_x", [P, 2, COLS])
        ps0 = psum("ps0", [P, 2, COLS])
        ps1 = psum("ps1", [P, 2, COLS])
        ps_top = psum("ps_top", [P, 2, COLS])

        ids_in = sem("ids_in")
        ident_in = sem("ident_in")
        w0_in = sem("w0_in")
        w1_in = sem("w1_in")
        top_in = sem("top_in")
        gathered = [sem(f"gathered{t}") for t in range(TILES)]
        w0_ready = sem("w0_ready")
        x_turned = sem("x_turned")
        x_copied = sem("x_copied")
        x_stored = [sem(f"x_stored{s}") for s in range(2)]
        shift_in = [sem(f"shift_in{s}") for s in range(2)]
        rep_in = [sem(f"rep_in{s}") for s in range(2)]
        cur0_rep_in = [sem(f"cur0_rep_in{s}") for s in range(2)]
        z0_ready = sem("z0_ready")
        l0_done = sem("l0_done")
        cur0_ready = sem("cur0_ready")
        cur0_stored = sem("cur0_stored")
        z1_ready = sem("z1_ready")
        z1_used = sem("z1_used")
        acc0_done = sem("acc0_done")
        acc1_done = sem("acc1_done")
        acc_zeroed = sem("acc_zeroed")
        pooled_ready = sem("pooled_ready")
        top_sum = sem("top_sum")
        top_act = sem("top_act")
        y_stored = sem("y_stored")

        block = ctx.enter_context(nc.Block())

        @block.gpsimd
        def _(pool):
            pool.wait_ge(ids_in, DMA)
            for t in range(TILES):
                for f in range(FIELDS):
                    nc.gpsimd.indirect_dma_start(
                        out=emb[:, t, f, :], out_offset=None, in_=tables[f],
                        in_offset=bass.IndirectOffsetOnAxis(
                            ap=ids_sb[:, t, f:f + 1].bitcast(U32), axis=0),
                    ).then_inc(gathered[t], DMA)

        @block.sync
        def _(sp):
            def store_x(half_tile, s):
                sp.wait_ge(x_copied, half_tile + 1)
                for twice in range(2):
                    for g in range(GROUPS):
                        sp.dma_start(
                            x_rows[half_tile * GROUPS + g, twice * FIELDS:(twice + 1) * FIELDS, :],
                            xt[g:P:GROUPS, s, :]).then_inc(x_stored[s], DMA)

            def copy_cur0(a, s):
                sp.wait_ge(cur0_ready, a + 1)
                sp.dma_start(cur0_rows[s], cur0[:, s, :]).then_inc(cur0_stored, DMA)
                sp.wait_ge(cur0_stored, (a + 1) * DMA)
                rows = cur0_rows[s].rearrange("(q j) c -> q (j c)", j=MJ)
                sp.dma_start(
                    cur0_rep[:, s].rearrange("p j c -> p (j c)"),
                    rows.unsqueeze(0).to_broadcast([HQ, MQ, MJ * COLS]),
                ).then_inc(cur0_rep_in[s], DMA)

            sp.dma_start(ids_sb[:], ids.rearrange("(t p) f -> p t f", p=P)).then_inc(ids_in, DMA)
            sp.dma_start(ident[:], identity).then_inc(ident_in, DMA)
            for sq in range(SHIFTS // ST):
                for a, src in ((w0a, w0_wide), (w0b, w0_tall)):
                    wide = src is w0_wide
                    step_h = (2 * FIELDS + 1) if wide else (FIELDS + 1)
                    step_s = 1 if wide else FIELDS
                    sp.dma_start(
                        a[sq * FIELDS:(sq + 1) * FIELDS],
                        bass.AP(src.tensor, ST * sq * step_s * MAPS,
                                [[step_h * MAPS, FIELDS], [step_s * MAPS, ST], [1, MAPS]]),
                    ).then_inc(w0_in, DMA)
            for a, src, step_h, step_s in ((w0a_last, w0_wide, 2 * FIELDS + 1, 1),
                                           (w0b_last, w0_tall, FIELDS + 1, FIELDS)):
                sp.dma_start(a, bass.AP(src.tensor, SHIFTS * step_s * MAPS,
                                           [[step_h * MAPS, SHIFTS], [1, MAPS]])).then_inc(w0_in, DMA)
            w1_v = w1.rearrange("o (hq i mq jm) n -> (o hq) mq i (jm n)", hq=HQ, i=HI, mq=MQ)
            for hq in range(HQ):
                sp.dma_start(w1_sb[hq * MQ:(hq + 1) * MQ].rearrange("p i j n -> p i (j n)"),
                             w1_v[hq]).then_inc(w1_in, DMA)

            store_x(0, 0)
            store_x(1, 1)
            copy_cur0(0, 0)
            copy_cur0(1, 1)
            with sp.Fori(0, 2) as k:
                copy_cur0(2 * k + 2, 0)
                copy_cur0(2 * k + 3, 1)
            for half_tile in range(2, 2 * TILES):
                store_x(half_tile, half_tile % 2)
            sp.dma_start(ctx_sb[:], dense_t).then_inc(top_in, DMA)
            sp.dma_start(wt1[:], w_top1[0:2 * P].rearrange("(k p) n -> p k n", p=P)).then_inc(top_in, DMA)
            sp.dma_start(wt1_ctx[:], w_top1[2 * P:2 * P + CTX]).then_inc(top_in, DMA)
            sp.dma_start(wt2[:], w_top2.rearrange("(k p) n -> p k n", p=P)).then_inc(top_in, DMA)
            with nc.allow_non_contiguous_dma(reason="a few hundred bias and column words"):
                sp.dma_start(wt3[:], w_top3.rearrange("(k p) o -> p (k o)", p=P)).then_inc(top_in, DMA)
                sp.dma_start(bt1[:], b_top1.rearrange("(k p) -> p k", p=P)).then_inc(top_in, DMA)
                sp.dma_start(bt2[:], b_top2.rearrange("(k p) -> p k", p=P)).then_inc(top_in, DMA)
            with sp.Fori(3, STRIPS // 2) as k:
                copy_cur0(2 * k, 0)
                copy_cur0(2 * k + 1, 1)
            sp.wait_ge(top_act, M1 + M2 + 1)
            sp.dma_start(out.rearrange("b o -> o b"), y_sb).then_inc(y_stored, DMA)
            sp.wait_ge(y_stored, DMA)

        @block.scalar
        def _(act):
            def wait_stored(s, fillings):
                act.wait_ge(x_stored[s], fillings * 2 * GROUPS * DMA)

            def copy_x(t, s, first):
                act.wait_ge(x_turned, 2 * t + s + 1)
                if not first:
                    wait_stored(s, t)
                nc.scalar.copy(xt[:, s, :], ps_x[:, s, :]).then_inc(x_copied, 1)

            def load_shift(a, s):
                rows = bass.ds(a, 1)
                src = x_rows[rows]
                for sq in range(SHIFTS // ST):
                    lo = x_rows[rows, ST * sq:ST * sq + 1, :].rearrange("o f c -> (o f) c")
                    run = bass.AP(lo.tensor, lo.offset, [[COLS, FIELDS], [1, ST * COLS]])
                    act.dma_start(x_shift[sq * FIELDS:(sq + 1) * FIELDS, s].rearrange("p t c -> p (t c)"),
                                  run).then_inc(shift_in[s], DMA)
                act.dma_start(x_four[:, s, :], src[:, 0:FIELDS, :].to_broadcast(
                    [SHIFTS // ST, FIELDS, COLS])).then_inc(shift_in[s], DMA)
                act.dma_start(x_far[:, s, :], src[:, SHIFTS:FIELDS, :].rearrange(
                    "o f c -> (o f) c")).then_inc(shift_in[s], DMA)

            def load_rep(a, s):
                lo = x_rows[bass.ds(a, 1), 0:1, :].rearrange("o f c -> (o f) c")
                act.dma_start(x_rep[:, s].rearrange("p i c -> p (i c)"),
                              bass.AP(lo.tensor, lo.offset,
                                      [[HI * COLS, HQ], [0, MQ], [1, HI * COLS]])).then_inc(rep_in[s], DMA)

            def step(a, s, next_shift=True, first=False):
                if next_shift:
                    act.wait_ge(z0_ready, a + 1)
                    load_shift(a + 2, s)
                if not first:
                    act.wait_ge(z1_ready, (a - 1) * MJ)
                    act.wait_ge(cur0_stored, (a - 1) * DMA)
                    act.wait_ge(acc0_done, a - 1)
                load_rep(a, s)
                act.wait_ge(l0_done, a + 1)
                nc.scalar.activation(cur0[:, s, :], ps0[:, s, :], ACT.Relu).then_inc(cur0_ready, 1)

            copy_x(0, 0, True)
            copy_x(0, 1, True)
            wait_stored(0, 1)
            wait_stored(1, 1)
            load_shift(0, 0)
            load_shift(1, 1)
            step(0, 0, first=True)
            step(1, 1, first=True)
            with act.Fori(0, 2) as k:
                step(2 * k + 2, 0)
                step(2 * k + 3, 1)
            with act.Fori(1, TILES) as t:
                copy_x(t, 0, False)
                copy_x(t, 1, False)
            wait_stored(0, TILES)
            wait_stored(1, TILES)
            with act.Fori(3, STRIPS // 2 - 1) as k:
                step(2 * k, 0)
                step(2 * k + 1, 1)
            step(STRIPS - 2, 0, next_shift=False)
            step(STRIPS - 1, 1, next_shift=False)
            act.wait_ge(top_in, 7 * DMA)
            for m in range(M1):
                act.wait_ge(top_sum, m + 1)
                nc.scalar.activation(h1[:, m, :], ps_top[:, m % 2, 0:B], ACT.Relu,
                                     bias=bt1[:, m:m + 1]).then_inc(top_act, 1)
            for m in range(M2):
                act.wait_ge(top_sum, M1 + m + 1)
                nc.scalar.activation(h2[:, m, :], ps_top[:, m % 2, 0:B], ACT.Relu,
                                     bias=bt2[:, m:m + 1]).then_inc(top_act, 1)
            act.wait_ge(top_sum, M1 + M2 + 1)
            nc.scalar.copy(y_sb, ps_top[0:1, 0, 0:B]).then_inc(top_act, 1)

        @block.vector
        def _(dve):
            def layer1_products(a, s, turn, first=False):
                dve.wait_ge(shift_in[s], (turn + 1) * (SHIFTS // ST + 2) * DMA)
                if not first:
                    dve.wait_ge(l0_done, a)
                nc.vector.tensor_tensor(
                    z0[:], x_shift[:, s], x_four[:, s].unsqueeze(1).to_broadcast([P, ST, COLS]), ALU.mult)
                nc.vector.tensor_tensor(z0_last[:], x_four[0:SHIFTS, s], x_far[:, s],
                                        ALU.mult).then_inc(z0_ready, 1)

            def layer2_product(c, s, j, first=False):
                if not (first and j < RING):
                    dve.wait_ge(z1_used, c * MJ + j - RING + 1)
                nc.vector.tensor_tensor(
                    z1[:, j % RING], x_rep[:, s], cur0_rep[:, s, j].unsqueeze(1).to_broadcast([P, HI, COLS]),
                    ALU.mult).then_inc(z1_ready, 1)

            def add_layer(layer, c, s, done, ready):
                dve.wait_ge(ready, c + 1 if layer == 0 else (c + 1) * MJ)
                dve.wait_ge(done, c)
                tile = acc[:, layer, bass.ds(c // (2 * GROUPS), 1), :].rearrange("p o c -> p (o c)")
                src = (cur0 if layer == 0 else ps1)[:, s, :]
                nc.vector.scalar_tensor_tensor(out=tile, in0=src, scalar=0.0, in1=tile,
                                               op0=ALU.max, op1=ALU.add).then_inc(done, 1)

            def step(a, s, turn, first=False, last=False):
                if not last:
                    layer1_products(a, s, turn)
                turn_c = turn if s == 1 else turn - 1
                c, sc = a - 1, 1 - s
                dve.wait_ge(rep_in[sc], (turn_c + 1) * DMA)
                dve.wait_ge(cur0_rep_in[sc], (turn_c + 1) * DMA)
                for j in range(MJ):
                    layer2_product(c, sc, j, first)
                    if j == RING and not first:
                        add_layer(1, a - 2, s, acc1_done, z1_used)
                    if j == RING + 1 and not last:
                        add_layer(0, a, s, acc0_done, cur0_ready)

            nc.vector.memset(acc[:], 0.0).then_inc(acc_zeroed, 1)
            dve.wait_ge(w0_in, (2 * SHIFTS // ST + 2) * DMA)
            nc.vector.memset(w0b[0:FIELDS, 0, :], 0.0).then_inc(acc_zeroed, 1)
            dve.wait_ge(acc_zeroed, 2)
            nc.vector.tensor_tensor(w0[:], w0a, w0b, ALU.add).then_inc(w0_ready, 1)
            nc.vector.tensor_tensor(w0_last[:], w0a_last, w0b_last, ALU.add).then_inc(w0_ready, 1)

            layer1_products(0, 0, 0, first=True)
            dve.wait_ge(cur0_ready, 1)
            nc.vector.tensor_copy(acc[:, 0, 0, :], cur0[:, 0, :]).then_inc(acc0_done, 1)
            step(1, 1, 0, first=True)
            with dve.Fori(1, STRIPS // 2) as k:
                step(2 * k, 0, k)
                step(2 * k + 1, 1, k)
            step(STRIPS, 0, STRIPS // 2, last=True)
            add_layer(1, STRIPS - 1, 1, acc1_done, z1_used)
            dve.wait_ge(acc0_done, STRIPS)
            dve.wait_ge(acc1_done, STRIPS)
            for layer in range(2):
                nc.vector.tensor_reduce(
                    pooled[:, layer, :].rearrange("p (t b) -> p t b", b=P),
                    acc[:, layer].rearrange("p t (d b) -> p t b d", b=P), AX.X,
                    ALU.add).then_inc(pooled_ready, 1)

        @block.tensor
        def _(pe):
            def turn_x(half_tile):
                t, half = half_tile // 2, half_tile % 2
                src = emb[:, t].rearrange("p f (g e) -> p e (f g)", g=GROUPS)
                if half_tile >= 2:
                    pe.wait_ge(x_copied, half_tile - 1)
                for e in range(HALF):
                    last = nc.tensor.transpose(ps_x[:, half, e * P:(e + 1) * P],
                                               src[:, half * HALF + e], ident[:])
                last.then_inc(x_turned, 1)

            def layer1(a, s, first=False):
                pe.wait_ge(z0_ready, a + 1)
                if not first:
                    pe.wait_ge(cur0_ready, a - 1)
                for t in range(ST):
                    nc.tensor.matmul(ps0[:, s, :], w0[:, t, :], z0[:, t, :], start=(t == 0), stop=False)
                nc.tensor.matmul(ps0[:, s, :], w0_last[:], z0_last[:], start=False,
                                 stop=True).then_inc(l0_done, 1)

            def layer2(c, s, first=False):
                if not first:
                    pe.wait_ge(acc1_done, c - 1)
                for j in range(MJ):
                    pe.wait_ge(z1_ready, c * MJ + j + 1)
                    for i in range(HI):
                        last = nc.tensor.matmul(ps1[:, s, :], w1_sb[:, i, j, :], z1[:, j % RING, i, :],
                                                start=(j == 0 and i == 0), stop=(j == MJ - 1 and i == HI - 1))
                    last.then_inc(z1_used, 1)

            def half_pair(k):
                layer1(2 * k + 1, 1)
                layer2(2 * k, 0)

            def pair(k):
                half_pair(k)
                layer1(2 * k + 2, 0)
                layer2(2 * k + 1, 1)

            pe.wait_ge(ident_in, DMA)
            pe.wait_ge(gathered[0], FIELDS * DMA)
            turn_x(0)
            turn_x(1)
            pe.wait_ge(w0_ready, 2)
            layer1(0, 0, first=True)
            pe.wait_ge(w1_in, HQ * DMA)
            layer1(1, 1, first=True)
            layer2(0, 0, first=True)
            layer1(2, 0)
            layer2(1, 1, first=True)
            pair(1)
            half_pair(2)
            for t in range(1, TILES):
                pe.wait_ge(gathered[t], FIELDS * DMA)
                turn_x(2 * t)
                turn_x(2 * t + 1)
            layer1(6, 0)
            layer2(5, 1)
            with pe.Fori(3, STRIPS // 2 - 1) as k:
                pair(k)
            layer1(STRIPS - 1, 1)
            layer2(STRIPS - 2, 0)
            layer2(STRIPS - 1, 1)

            pe.wait_ge(top_in, 7 * DMA)
            pe.wait_ge(pooled_ready, 2)
            for m in range(M1):
                cols = slice(m * P, (m + 1) * P)
                if m >= 2:
                    pe.wait_ge(top_act, m - 1)
                bank = ps_top[:, m % 2, 0:B]
                nc.tensor.matmul(bank, wt1[:, 0, cols], pooled[:, 0, :], start=True, stop=False)
                nc.tensor.matmul(bank, wt1[:, 1, cols], pooled[:, 1, :], start=False, stop=False)
                nc.tensor.matmul(bank, wt1_ctx[:, cols], ctx_sb[:], start=False, stop=True).then_inc(top_sum, 1)
            for m in range(M2):
                pe.wait_ge(top_act, M1)
                for k in range(M1):
                    last = nc.tensor.matmul(ps_top[:, m % 2, 0:B], wt2[:, k, m * P:(m + 1) * P], h1[:, k, :],
                                            start=(k == 0), stop=(k == M1 - 1))
                last.then_inc(top_sum, 1)
            pe.wait_ge(top_act, M1 + M2)
            for k in range(M2):
                last = nc.tensor.matmul(ps_top[0:1, 0, 0:B], wt3[:, k:k + 1], h2[:, k, :],
                                        start=(k == 0), stop=(k == M2 - 1))
            last.then_inc(top_sum, 1)


def kernel(**inputs):
    import numpy as np
    import concourse.bacc as bacc
    from concourse.bass_utils import run_bass_kernel_spmd

    nc = bacc.Bacc("TRN2", target_bir_lowering=False, num_devices=1)
    arrays = {}

    def dram_in(name, a):
        a = np.ascontiguousarray(a)
        arrays[name] = a
        return nc.dram_tensor(name, a.shape, mybir.dt.from_np(a.dtype), kind="ExternalInput").ap()

    filter_0 = np.asarray(inputs["L0_rec_filter_0"]).reshape(FIELDS, FIELDS, MAPS)
    dense_t = dram_in("dense_t", np.asarray(inputs["dense_ctx"]).T)
    ids = dram_in("ids_in", inputs["ids"])
    tables = [dram_in(f"tbl_{f}", inputs[f"tbl_{f}"]) for f in range(FIELDS)]
    top = [dram_in(n, inputs[n]) for n in ("W_top1", "b_top1", "W_top2", "b_top2", "W_top3")]
    w0_wide = dram_in("w0_wide", np.concatenate([filter_0, filter_0], axis=1))
    w0_tall = dram_in("w0_tall", np.concatenate([filter_0, filter_0], axis=0))
    w1 = dram_in("w1", inputs["L0_rec_filter_1"])
    identity = dram_in("identity", np.eye(P, dtype=np.float32))
    out = nc.dram_tensor("y", (inputs["ids"].shape[0], 1), F32, kind="ExternalOutput").ap()
    build_cin_tower(nc, dense_t, ids, tables, *top, w0_wide, w0_tall, w1, identity, out)
    r = run_bass_kernel_spmd(nc, [arrays], core_ids=[0])
    return r.results[0]["y"]
```

```python
from contextlib import ExitStack

import concourse.bass as bass
from concourse import mybir

F32 = mybir.dt.float32
F32R = mybir.dt.float32r
I32 = mybir.dt.int32
U32 = mybir.dt.uint32
ALU = mybir.AluOpType
ACT = mybir.ActivationFunctionType

P = 128
FIELDS = 32
DIM = 32
MAPS = 128
GROUPS = 4
PER_GROUP = DIM // GROUPS
BLOCKS = PER_GROUP // 2
COLS = BLOCKS * P
PER_TILE = 2 * GROUPS
SHIFTS = 16
ST = 4
QUAD = 4
QUADS = FIELDS // QUAD
SCALED = 4
SUMMED = QUADS - SCALED
ACT_BANKS = 2
VEC_BANKS = 4
W1_PARTS = 4
EARLY = 52
GATHERS = 4
DMA = 16


def build_cin_tower(nc: bass.Bass, dense_t, ids, tables, w_top1, b_top1, w_top2, b_top2, w_top3,
                    w0_wide, w0_tall, w1, identity, out):
    B = ids.shape[0]
    TILES = B // P
    STRIPS = TILES * PER_TILE
    CTX = dense_t.shape[0]
    N1, N2 = w_top1.shape[1], w_top2.shape[1]
    M1, M2 = N1 // P, N2 // P

    x_rows = nc.dram_tensor("x_rows", [STRIPS, 2 * FIELDS, COLS], F32).ap()

    with ExitStack() as ctx:
        def sb(name, shape, dt=F32):
            return ctx.enter_context(nc.sbuf_tensor(name, shape, dt))

        def psum(name, shape):
            return ctx.enter_context(nc.psum_tensor(name, shape, F32))

        def sem(name):
            return ctx.enter_context(nc.semaphore(name))

        ids_sb = sb("ids_sb", [P, TILES, FIELDS], I32)
        emb = sb("emb", [P, TILES * FIELDS * DIM])
        ident = sb("ident", [P, P])
        xt = sb("xt", [P, 2, COLS])
        w0a, w0b = sb("w0a", [P, ST, MAPS]), sb("w0b", [P, ST, MAPS])
        w0_far_raw = sb("w0_far_raw", [3 * FIELDS, MAPS])
        w0 = sb("w0", [P, ST, MAPS])
        w0_far = sb("w0_far", [3 * FIELDS, MAPS], F32R)
        w1_raw = sb("w1_raw", [P, FIELDS * MAPS])
        w1_hi = sb("w1_hi", [P, FIELDS * MAPS], F32R)
        w1_lo = sb("w1_lo", [P, FIELDS * MAPS], F32R)
        x_shift = sb("x_shift", [P, ST, COLS])
        x_four = sb("x_four", [P, COLS])
        x_far = sb("x_far", [3 * FIELDS, COLS])
        z = sb("z", [P, ST, COLS])
        far_whole = sb("far_whole", [3 * FIELDS, COLS])
        far = sb("far", [3 * FIELDS, COLS], F32R)
        cur0_hi = sb("cur0_hi", [P, 2, COLS], F32R)
        cur0_lo = sb("cur0_lo", [P, 2, COLS], F32R)
        xs = sb("xs", [P, 2, FIELDS, BLOCKS])
        scaled = sb("scaled", [P, 2, SCALED, QUAD, MAPS])
        part = sb("part", [P, 2, QUAD, MAPS])
        chain = sb("chain", [P, 2, QUAD, MAPS])
        fold_sb = sb("fold_sb", [P, 2, MAPS])
        cur1 = sb("cur1", [P, 2, BLOCKS, MAPS])
        acc0 = sb("acc0", [P, TILES, COLS])
        acc1 = sb("acc1", [P, TILES, COLS])
        pooled1_t = sb("pooled1_t", [P, TILES, MAPS])
        pooled = sb("pooled", [P, 2, B])
        ctx_sb = sb("ctx_sb", [CTX, B])
        wt1 = sb("wt1", [P, 2, N1])
        wt1_ctx = sb("wt1_ctx", [CTX, N1])
        wt2 = sb("wt2", [P, M1, N2])
        wt3 = sb("wt3", [P, M2])
        bt1 = sb("bt1", [P, M1])
        bt2 = sb("bt2", [P, M2])
        h1 = sb("h1", [P, M1, B])
        h2 = sb("h2", [P, M2, B])
        y_sb = sb("y_sb", [1, B])

        ps_x = psum("ps_x", [P, COLS])
        ps0 = psum("ps0", [P, COLS])
        act_sums = psum("act_sums", [P, ACT_BANKS, QUAD * MAPS])
        vec_sums = psum("vec_sums", [P, VEC_BANKS, QUAD * MAPS])
        ps_h1, ps_h2, ps_pooled, ps_y = vec_sums, act_sums, ps0, ps_x

        ids_in = sem("ids_in")
        ident_in = sem("ident_in")
        w0_in = sem("w0_in")
        w1_in = [sem(f"w1_in{i}") for i in range(W1_PARTS)]
        top_in = sem("top_in")
        gathered = [sem(f"gathered{t}") for t in range(TILES)]
        w0_high = sem("w0_high")
        w1_high = sem("w1_high")
        w0_ready = sem("w0_ready")
        w1_ready = sem("w1_ready")
        cleared = sem("cleared")
        x_turned = sem("x_turned")
        x_copied = sem("x_copied")
        x_stored = [sem(f"x_stored{s}") for s in range(2)]
        shift_in = sem("shift_in")
        z_ready = sem("z_ready")
        far_whole_ready = sem("far_whole_ready")
        far_hi_ready = sem("far_hi_ready")
        far_ready = sem("far_ready")
        l0_done = sem("l0_done")
        cur0_hi_ready = sem("cur0_hi_ready")
        cur0_lo_ready = sem("cur0_lo_ready")
        xs_ready = sem("xs_ready")
        act_sums_ready = sem("act_sums_ready")
        vec_sums_ready = sem("vec_sums_ready")
        act_scaled = sem("act_scaled")
        vec_added = sem("vec_added")
        part_added = sem("part_added")
        folded = sem("folded")
        acc0_done = sem("acc0_done")
        acc1_done = sem("acc1_done")
        pooling = sem("pooling")
        pooled0_ready = sem("pooled0_ready")
        pooled1_t_ready = sem("pooled1_t_ready")
        pooled1_turned = sem("pooled1_turned")
        pooled1_ready = sem("pooled1_ready")
        h1_sum, h2_sum, y_sum = sem("h1_sum"), sem("h2_sum"), sem("y_sum")
        h1_ready, h2_ready, y_ready = sem("h1_ready"), sem("h2_ready"), sem("y_ready")
        y_stored = sem("y_stored")

        W0_DMAS = 2 * SHIFTS // ST + 1
        TOP_DMAS = 7
        SHIFT_DMAS = 3
        VEC_UNITS = SUMMED * BLOCKS
        ADDS = SCALED - 1
        PART = FIELDS * MAPS // W1_PARTS
        assert (SCALED * BLOCKS) % ACT_BANKS == 0 and VEC_UNITS % VEC_BANKS == 0
        assert EARLY >= FIELDS

        def is_number(a, below):
            return isinstance(a, int) and a < below

        def turned_in(a):
            if isinstance(a, int) and a % PER_TILE >= PER_TILE - 2 and a // PER_TILE + 1 < TILES:
                return 2 * (a // PER_TILE + 1) + a % PER_TILE - (PER_TILE - 2)
            return None

        def all_steps(eng, step):
            for a in range(1, PER_TILE):
                step(a, a % 2)
            for t in range(1, TILES):
                first = t * PER_TILE // 2
                with eng.Fori(first, first + PER_TILE // 2 - 1) as k:
                    step(2 * k, 0, t)
                    step(2 * k + 1, 1, t)
                step(t * PER_TILE + PER_TILE - 2, 0)
                step(t * PER_TILE + PER_TILE - 1, 1)

        block = ctx.enter_context(nc.Block())

        @block.gpsimd
        def _(pool):
            def gather(n):
                t, f = n // FIELDS, n % FIELDS
                at = n * DIM
                nc.gpsimd.indirect_dma_start(
                    out=emb[:, at:at + DIM], out_offset=None, in_=tables[f],
                    in_offset=bass.IndirectOffsetOnAxis(ap=ids_sb[:, t, f:f + 1].bitcast(U32), axis=0),
                ).then_inc(gathered[t], DMA)

            def add_part(b, sb, n):
                pool.wait_ge(act_scaled, SCALED * b + n + 2)
                if n > 0:
                    pool.wait_ge(part_added, ADDS * b + n)
                elif not is_number(b, 2):
                    pool.wait_ge(vec_added, QUAD * (SUMMED * (b - 2) + 1))
                nc.gpsimd.tensor_tensor(part[:, sb], scaled[:, sb, 0] if n == 0 else part[:, sb],
                                        scaled[:, sb, n + 1], ALU.add).then_inc(part_added, 1)

            def fold(c, sc, e, n):
                b = BLOCKS * c + e
                sb = e % 2
                if n == 0:
                    pool.wait_ge(vec_added, QUAD * SUMMED * (b + 1))
                    if not is_number(b, 1):
                        pool.wait_ge(folded, 2 * b)
                    nc.gpsimd.tensor_tensor(fold_sb[:], chain[:, sb, 0:2], chain[:, sb, 2:4],
                                            ALU.add).then_inc(folded, 1)
                else:
                    pool.wait_ge(folded, 2 * b + 1)
                    if e == 0 and not is_number(c, 2):
                        pool.wait_ge(acc1_done, c - 1)
                    nc.gpsimd.tensor_tensor(cur1[:, sc, e], fold_sb[:, 0], fold_sb[:, 1],
                                            ALU.add).then_inc(folded, 1)

            def step(a, s, gathers=()):
                c = a - 1
                for e in range(BLOCKS):
                    if e < len(gathers):
                        gather(gathers[e])
                    ahead = BLOCKS * c + e + 1
                    no_ahead = isinstance(a, int) and a == STRIPS and e == BLOCKS - 1
                    behind = c if e > 0 else c - 1
                    for n in range(ADDS):
                        if not no_ahead:
                            add_part(ahead, (e + 1) % 2, n)
                        if not is_number(behind, 0) and n < 2:
                            fold(behind, 1 - s if e > 0 else s, (e - 1) % BLOCKS, n)

            pool.wait_ge(ids_in, DMA)
            for n in range(EARLY):
                gather(n)
            for n in range(ADDS):
                add_part(0, 0, n)
            done = EARLY
            total = TILES * FIELDS
            looped = 2 * -(-(1 + -(-(total - EARLY) // GATHERS)) // 2)
            for a in range(1, looped):
                step(a, a % 2, range(done, min(done + GATHERS, total)))
                done += GATHERS
            with pool.Fori(looped // 2, STRIPS // 2) as k:
                step(2 * k, 0)
                step(2 * k + 1, 1)
            step(STRIPS, 0)
            for n in range(2):
                fold(STRIPS - 1, 1, BLOCKS - 1, n)

        @block.sync
        def _(sp):
            def store_x(half_tile):
                t, half = half_tile // 2, half_tile % 2
                sp.wait_ge(x_copied, half_tile + 1)
                strips = x_rows[t * PER_TILE:(t + 1) * PER_TILE].rearrange(
                    "(g two) f c -> two g f c", two=2)[half]
                for twice in range(2):
                    sp.dma_start(strips[:, twice * FIELDS:(twice + 1) * FIELDS, :].rearrange("g f c -> f g c"),
                                 xt[:, half, :]).then_inc(x_stored[half], DMA)

            def load_shift(a, t, s):
                sp.wait_ge(x_stored[s], (t + 1) * 2 * DMA)
                first = x_rows[bass.ds(a, 1), 0:1, :].rearrange("o f c -> (o f) c")
                sp.dma_start(x_shift[:].rearrange("p t c -> p (t c)"),
                             bass.AP(first.tensor, first.offset,
                                     [[ST * COLS, SHIFTS // ST], [COLS, FIELDS], [1, ST * COLS]]),
                             ).then_inc(shift_in, DMA)
                sp.dma_start(x_four[:], bass.AP(first.tensor, first.offset,
                                                [[0, SHIFTS // ST], [COLS, FIELDS], [1, COLS]]),
                             ).then_inc(shift_in, DMA)
                sp.dma_start(x_far[:], bass.AP(first.tensor, first.offset + SHIFTS * COLS,
                                               [[0, 3], [COLS, FIELDS], [1, COLS]]),
                             ).then_inc(shift_in, DMA)

            def step(a, s, tile=None):
                turn = turned_in(a)
                if turn is not None:
                    store_x(turn)
                if isinstance(a, int) and a == STRIPS - 1:
                    return
                sp.wait_ge(far_whole_ready, a + 1)
                load_shift(a + 1, (a + 1) // PER_TILE if isinstance(a, int) else tile, 1 - s)

            sp.dma_start(ids_sb[:], ids.rearrange("(t p) f -> p t f", p=P)).then_inc(ids_in, DMA)
            sp.dma_start(ident[:], identity).then_inc(ident_in, DMA)
            for sq in range(SHIFTS // ST):
                for a, src, step_h, step_s in ((w0a, w0_wide, 2 * FIELDS + 1, 1),
                                               (w0b, w0_tall, FIELDS + 1, FIELDS)):
                    sp.dma_start(
                        a[sq * FIELDS:(sq + 1) * FIELDS],
                        bass.AP(src.tensor, ST * sq * step_s * MAPS,
                                [[step_h * MAPS, FIELDS], [step_s * MAPS, ST], [1, MAPS]]),
                    ).then_inc(w0_in, DMA)
            sp.dma_start(w0_far_raw[:], bass.AP(w0_wide.tensor, SHIFTS * MAPS,
                                                [[0, 3], [(2 * FIELDS + 1) * MAPS, FIELDS], [1, MAPS]]),
                         ).then_inc(w0_in, DMA)
            w1_v = w1.rearrange("o (h m) n -> (o m) h n", m=MAPS)
            per = FIELDS // W1_PARTS
            for i in range(W1_PARTS):
                sp.dma_start(w1_raw[:, i * PART:(i + 1) * PART].rearrange("p (h n) -> p h n", n=MAPS),
                             w1_v[:, i * per:(i + 1) * per, :]).then_inc(w1_in[i], DMA)
            store_x(0)
            load_shift(0, 0, 0)
            store_x(1)
            sp.wait_ge(far_whole_ready, 1)
            load_shift(1, 0, 1)
            sp.dma_start(ctx_sb[:], dense_t).then_inc(top_in, DMA)
            sp.dma_start(wt1[:], w_top1[0:2 * P].rearrange("(k p) n -> p k n", p=P)).then_inc(top_in, DMA)
            sp.dma_start(wt1_ctx[:], w_top1[2 * P:2 * P + CTX]).then_inc(top_in, DMA)
            sp.dma_start(wt2[:], w_top2.rearrange("(k p) n -> p k n", p=P)).then_inc(top_in, DMA)
            with nc.allow_non_contiguous_dma(reason="a few hundred bias and column words"):
                sp.dma_start(wt3[:], w_top3.rearrange("(k p) o -> p (k o)", p=P)).then_inc(top_in, DMA)
                sp.dma_start(bt1[:], b_top1.rearrange("(k p) -> p k", p=P)).then_inc(top_in, DMA)
                sp.dma_start(bt2[:], b_top2.rearrange("(k p) -> p k", p=P)).then_inc(top_in, DMA)
            all_steps(sp, step)
            sp.wait_ge(y_ready, 1)
            sp.dma_start(out.rearrange("b o -> o b"), y_sb[:]).then_inc(y_stored, DMA)
            sp.wait_ge(y_stored, DMA)

        @block.scalar
        def _(act):
            def copy_x(half_tile):
                act.wait_ge(x_turned, half_tile + 1)
                t, half = half_tile // 2, half_tile % 2
                if t > 0:
                    act.wait_ge(x_stored[half], t * 2 * DMA)
                nc.scalar.copy(xt[:, half, :], ps_x[:]).then_inc(x_copied, 1)

            def take_cur0(a, s):
                act.wait_ge(l0_done, a + 1)
                nc.scalar.activation(cur0_hi[:, s, :], ps0[:], ACT.Relu).then_inc(cur0_hi_ready, 1)

            def take_xs(a, s, tile):
                if not is_number(a, 2):
                    act.wait_ge(vec_added, QUAD * VEC_UNITS * (a - 1))
                    act.wait_ge(act_scaled, SCALED * BLOCKS * (a - 1))
                if isinstance(a, int):
                    at = FIELDS * DIM * (a // PER_TILE) + BLOCKS * (a % PER_TILE)
                    rows = emb[:, at:at + (FIELDS - 1) * DIM + BLOCKS]
                    act.wait_ge(gathered[a // PER_TILE], FIELDS * DMA)
                else:
                    at = tile * FIELDS * DIM + (a - tile * PER_TILE) * BLOCKS
                    rows = emb[:, bass.ds(at, (FIELDS - 1) * DIM + BLOCKS)]
                first = rows[:, 0:1]
                nc.scalar.copy(xs[:, s], bass.AP(first.tensor, first.offset,
                                                 [first.ap[0], [DIM, FIELDS], [1, BLOCKS]])
                               ).then_inc(xs_ready, 1)

            def scale_quad(b, sc, e, n):
                bank = (SCALED * e + n) % ACT_BANKS
                act.wait_ge(act_sums_ready, SCALED * b + n + 1)
                if not is_number(b, 2):
                    act.wait_ge(part_added, ADDS * (b - 1))
                for i in range(QUAD):
                    last = nc.scalar.activation(scaled[:, e % 2, n, i, :],
                                                act_sums[:, bank, i * MAPS:(i + 1) * MAPS], ACT.Copy,
                                                scale=xs[:, sc, QUAD * n + i, e:e + 1])
                last.then_inc(act_scaled, 1)

            def far_high(a):
                if not is_number(a, 1):
                    act.wait_ge(l0_done, a)
                act.wait_ge(far_whole_ready, a + 1)
                nc.scalar.copy(far[:], far_whole[:]).then_inc(far_hi_ready, 1)

            def step(a, s, tile=None):
                c = a - 1
                last = isinstance(a, int) and a == STRIPS
                turn = turned_in(a)
                if turn is not None:
                    copy_x(turn)
                if not last:
                    take_cur0(a, s)
                for e in range(1, BLOCKS):
                    for n in range(SCALED):
                        scale_quad(BLOCKS * c + e, 1 - s, e, n)
                    if e == 1 and not last:
                        take_xs(a, s, tile)
                    if e == 3 and not (isinstance(a, int) and a >= STRIPS - 1):
                        far_high(a + 1)
                if not last:
                    act.wait_ge(xs_ready, a + 1)
                    for n in range(SCALED):
                        scale_quad(BLOCKS * a, s, 0, n)

            act.wait_ge(w0_in, W0_DMAS * DMA)
            nc.scalar.copy(w0_far[:], w0_far_raw[:]).then_inc(w0_high, 1)
            for i in range(W1_PARTS):
                cols = slice(i * PART, (i + 1) * PART)
                act.wait_ge(w1_in[i], DMA)
                nc.scalar.copy(w1_hi[:, cols], w1_raw[:, cols]).then_inc(w1_high, 1)
            copy_x(0)
            copy_x(1)
            take_xs(0, 0, 0)
            far_high(0)
            take_cur0(0, 0)
            act.wait_ge(xs_ready, 1)
            for n in range(SCALED):
                scale_quad(0, 0, 0, n)
            far_high(1)
            all_steps(act, step)
            step(STRIPS, 0)
            act.wait_ge(pooled1_turned, TILES)
            nc.scalar.copy(pooled[:, 1, :], ps_pooled[:, 0:B]).then_inc(pooled1_ready, 1)
            act.wait_ge(top_in, TOP_DMAS * DMA)
            for m in range(M1):
                act.wait_ge(h1_sum, m + 1)
                nc.scalar.activation(h1[:, m, :], ps_h1[:, m, 0:B], ACT.Relu,
                                     bias=bt1[:, m:m + 1]).then_inc(h1_ready, 1)
            for m in range(M2):
                act.wait_ge(h2_sum, m + 1)
                nc.scalar.activation(h2[:, m, :], ps_h2[:, m, 0:B], ACT.Relu,
                                     bias=bt2[:, m:m + 1]).then_inc(h2_ready, 1)
            act.wait_ge(y_sum, 1)
            nc.scalar.copy(y_sb[:], ps_y[0:1, 0:B]).then_inc(y_ready, 1)

        @block.vector
        def _(dve):
            def layer1_product(a, t):
                if t == 0:
                    dve.wait_ge(shift_in, (a + 1) * SHIFT_DMAS * DMA)
                    if not is_number(a, 1):
                        dve.wait_ge(l0_done, a)
                nc.vector.tensor_tensor(z[:, t], x_shift[:, t], x_four[:], ALU.mult).then_inc(z_ready, 1)

            def far_product(a):
                if not is_number(a, 1):
                    dve.wait_ge(far_ready, a)
                nc.vector.tensor_tensor(far_whole[:], x_far[:], x_four[0:3 * FIELDS],
                                        ALU.mult).then_inc(far_whole_ready, 1)

            def far_low(a):
                dve.wait_ge(far_hi_ready, a + 1)
                low = slice(2 * FIELDS, 3 * FIELDS)
                nc.vector.tensor_tensor(far[low], far_whole[low], far[low],
                                        ALU.subtract).then_inc(far_ready, 1)

            def take_cur0(a, s, t):
                dve.wait_ge(cur0_hi_ready, a + 1)
                nc.vector.scalar_tensor_tensor(out=cur0_lo[:, s, :], in0=ps0[:], scalar=0.0,
                                               in1=cur0_hi[:, s, :].bitcast(F32), op0=ALU.max,
                                               op1=ALU.subtract).then_inc(cur0_lo_ready, 1)
                add(acc0, acc0_done, a, ps0[:])

            def tile_of(acc, a):
                if isinstance(a, int):
                    return acc[:, a // PER_TILE, :]
                at = (a & (STRIPS - PER_TILE)) * (COLS // PER_TILE)
                return acc[:].rearrange("p t c -> p (t c)")[:, bass.ds(at, COLS)]

            def add(acc, done, a, sums):
                if not is_number(a, 1):
                    dve.wait_ge(done, a)
                into = tile_of(acc, a)
                nc.vector.scalar_tensor_tensor(out=into, in0=sums, scalar=0.0, in1=into, op0=ALU.max,
                                               op1=ALU.add).then_inc(done, 1)

            def add1(c, s):
                dve.wait_ge(folded, 2 * BLOCKS * (c + 1))
                add(acc1, acc1_done, c, cur1[:, s].rearrange("p e n -> p (e n)"))

            def add_quad(c, sc, e, n):
                b = BLOCKS * c + e
                unit = VEC_UNITS * c + SUMMED * e + n
                sb = e % 2
                bank = (SUMMED * e + n) % VEC_BANKS
                dve.wait_ge(vec_sums_ready, unit + 1)
                if n == 0:
                    dve.wait_ge(part_added, ADDS * (b + 1))
                    if not is_number(b, 2):
                        dve.wait_ge(folded, 2 * (b - 2) + 1)
                for i in range(QUAD):
                    if n > 0 and i in (0, 2):
                        dve.wait_ge(vec_added, QUAD * unit + i - 2)
                    nc.vector.scalar_tensor_tensor(
                        out=chain[:, sb, i, :], in0=vec_sums[:, bank, i * MAPS:(i + 1) * MAPS],
                        scalar=xs[:, sc, QUAD * (SCALED + n) + i, e:e + 1],
                        in1=part[:, sb, i, :] if n == 0 else chain[:, sb, i, :],
                        op0=ALU.mult, op1=ALU.add).then_inc(vec_added, 1)

            def step(a, s, tile=None):
                c = a - 1
                last = isinstance(a, int) and a == STRIPS
                dve.wait_ge(xs_ready, a)
                for e in range(BLOCKS):
                    for n in range(SUMMED):
                        add_quad(c, 1 - s, e, n)
                        if e == 0 and n == 2 and not last:
                            take_cur0(a, s, None)
                        if isinstance(a, int) and a >= STRIPS - 1:
                            continue
                        if e == 1:
                            layer1_product(a + 1, n)
                        if e == 2 and n == 0:
                            far_product(a + 1)
                        if e == 3 and n == 2:
                            far_low(a + 1)
                    if e == 0 and not is_number(a, 2):
                        add1(a - 2, s)

            def pool_dims(acc, done, tiles, into, ready):
                dve.wait_ge(done, PER_TILE * tiles.stop)
                nc.vector.tensor_tensor(acc[:, tiles, 0:2 * P], acc[:, tiles, 0:2 * P],
                                        acc[:, tiles, 2 * P:4 * P], ALU.add).then_inc(pooling, 1)
                pool_dims.steps += 1
                dve.wait_ge(pooling, pool_dims.steps)
                nc.vector.tensor_tensor(into, acc[:, tiles, 0:P], acc[:, tiles, P:2 * P],
                                        ALU.add).then_inc(ready, 1)

            pool_dims.steps = 0
            nc.vector.memset(acc0[:], 0.0).then_inc(cleared, 1)
            nc.vector.memset(acc1[:], 0.0).then_inc(cleared, 1)
            dve.wait_ge(w0_in, W0_DMAS * DMA)
            nc.vector.memset(w0b[0:FIELDS, 0, :], 0.0).then_inc(w0_ready, 1)
            dve.wait_ge(w0_ready, 1)
            nc.vector.tensor_tensor(w0[:], w0a[:], w0b[:], ALU.add).then_inc(w0_ready, 1)
            dve.wait_ge(w0_high, 1)
            low = slice(FIELDS, 2 * FIELDS)
            nc.vector.tensor_tensor(w0_far[low], w0_far_raw[low], w0_far[low],
                                    ALU.subtract).then_inc(w0_ready, 1)
            for i in range(W1_PARTS):
                cols = slice(i * PART, (i + 1) * PART)
                dve.wait_ge(w1_high, i + 1)
                nc.vector.tensor_tensor(w1_lo[:, cols], w1_raw[:, cols], w1_hi[:, cols],
                                        ALU.subtract).then_inc(w1_ready, 1)
            dve.wait_ge(cleared, 2)
            for t in range(ST):
                layer1_product(0, t)
            far_product(0)
            far_low(0)
            take_cur0(0, 0, 0)
            for t in range(ST):
                layer1_product(1, t)
            far_product(1)
            far_low(1)
            all_steps(dve, step)
            step(STRIPS, 0)
            rows = pooled[:, 0, :].rearrange("p (t b) -> p t b", t=TILES)
            pool_dims(acc0, acc0_done, slice(0, TILES), rows, pooled0_ready)
            pool_dims(acc1, acc1_done, slice(0, TILES - 1), pooled1_t[:, 0:TILES - 1], pooled1_t_ready)
            add1(STRIPS - 1, 1)
            pool_dims(acc1, acc1_done, slice(TILES - 1, TILES), pooled1_t[:, TILES - 1:TILES],
                      pooled1_t_ready)

        @block.tensor
        def _(pe):
            def turn_x(half_tile):
                t, half = half_tile // 2, half_tile % 2
                pe.wait_ge(gathered[t], FIELDS * DMA)
                src = emb[:, t * FIELDS * DIM:(t + 1) * FIELDS * DIM].rearrange(
                    "p (fg e) -> p e fg", e=PER_GROUP)
                if half_tile > 0:
                    pe.wait_ge(x_copied, half_tile)
                for e in range(BLOCKS):
                    last = nc.tensor.transpose(ps_x[:, e * P:(e + 1) * P], src[:, half * BLOCKS + e],
                                               ident[:])
                last.then_inc(x_turned, 1)

            def layer1(a):
                pe.wait_ge(z_ready, ST * (a + 1))
                if not is_number(a, 1):
                    pe.wait_ge(acc0_done, a)
                for t in range(ST):
                    nc.tensor.matmul(ps0[:], w0[:, t, :], z[:, t, :], start=(t == 0), stop=False)
                pe.wait_ge(far_ready, a + 1)
                nc.tensor.matmul(ps0[:], w0_far[:], far[:], start=False, stop=True).then_inc(l0_done, 1)

            def quad(bank, sc, e, q):
                cols, maps = slice(e * P, (e + 1) * P), slice(q * QUAD * MAPS, (q + 1) * QUAD * MAPS)
                hi, lo = cur0_hi[:, sc, cols], cur0_lo[:, sc, cols]
                nc.tensor.matmul(bank, hi, w1_lo[:, maps], start=True, stop=False)
                nc.tensor.matmul(bank, hi, w1_hi[:, maps], start=False, stop=False)
                return nc.tensor.matmul(bank, lo, w1_hi[:, maps], start=False, stop=True)

            def quad_for_act(b, sc, e, n):
                unit = SCALED * b + n
                if not is_number(unit, ACT_BANKS):
                    pe.wait_ge(act_scaled, unit - ACT_BANKS + 1)
                quad(act_sums[:, (SCALED * e + n) % ACT_BANKS, :], sc, e, n).then_inc(act_sums_ready, 1)

            def quad_for_vec(c, sc, e, n):
                unit = VEC_UNITS * c + SUMMED * e + n
                if not is_number(unit, VEC_BANKS):
                    pe.wait_ge(vec_added, QUAD * (unit - VEC_BANKS + 1))
                quad(vec_sums[:, (SUMMED * e + n) % VEC_BANKS, :], sc, e,
                     SCALED + n).then_inc(vec_sums_ready, 1)

            def step(a, s, tile=None):
                c = a - 1
                last = isinstance(a, int) and a == STRIPS
                turn = turned_in(a)
                if turn is not None:
                    turn_x(turn)
                if not last:
                    layer1(a)
                for e in range(BLOCKS):
                    if e == BLOCKS - 1 and not last:
                        pe.wait_ge(cur0_lo_ready, a + 1)
                    for n in range(max(SCALED, SUMMED)):
                        if n < SUMMED:
                            quad_for_vec(c, 1 - s, e, n)
                        if n < SCALED and e < BLOCKS - 1:
                            quad_for_act(BLOCKS * c + e + 1, 1 - s, e + 1, n)
                        elif n < SCALED and not last:
                            quad_for_act(BLOCKS * a, s, 0, n)

            pe.wait_ge(ident_in, DMA)
            turn_x(0)
            turn_x(1)
            pe.wait_ge(w0_ready, 3)
            layer1(0)
            pe.wait_ge(w1_ready, W1_PARTS)
            pe.wait_ge(cur0_lo_ready, 1)
            for n in range(SCALED):
                quad_for_act(0, 0, 0, n)
            all_steps(pe, step)
            step(STRIPS, 0)

            pe.wait_ge(top_in, TOP_DMAS * DMA)
            pe.wait_ge(pooled0_ready, 1)
            for m in range(M1):
                cols = slice(m * P, (m + 1) * P)
                nc.tensor.matmul(ps_h1[:, m, 0:B], wt1_ctx[:, cols], ctx_sb[:], start=True, stop=False)
                nc.tensor.matmul(ps_h1[:, m, 0:B], wt1[:, 0, cols], pooled[:, 0, :], start=False,
                                 stop=False)
            for t in range(TILES):
                pe.wait_ge(pooled1_t_ready, 2 if t == TILES - 1 else 1)
                nc.tensor.transpose(ps_pooled[:, t * P:(t + 1) * P], pooled1_t[:, t, :],
                                    ident[:]).then_inc(pooled1_turned, 1)
            pe.wait_ge(pooled1_ready, 1)
            for m in range(M1):
                nc.tensor.matmul(ps_h1[:, m, 0:B], wt1[:, 1, m * P:(m + 1) * P], pooled[:, 1, :],
                                 start=False, stop=True).then_inc(h1_sum, 1)
            pe.wait_ge(act_scaled, SCALED * BLOCKS * STRIPS)
            for k in range(M1):
                pe.wait_ge(h1_ready, k + 1)
                for m in range(M2):
                    one = nc.tensor.matmul(ps_h2[:, m, 0:B], wt2[:, k, m * P:(m + 1) * P], h1[:, k, :],
                                           start=(k == 0), stop=(k == M1 - 1))
                    if k == M1 - 1:
                        one.then_inc(h2_sum, 1)
            for k in range(M2):
                pe.wait_ge(h2_ready, k + 1)
                last = nc.tensor.matmul(ps_y[0:1, 0:B], wt3[:, k:k + 1], h2[:, k, :],
                                        start=(k == 0), stop=(k == M2 - 1))
            last.then_inc(y_sum, 1)


def kernel(**inputs):
    import numpy as np
    import concourse.bacc as bacc
    from concourse.bass_utils import run_bass_kernel_spmd

    nc = bacc.Bacc("TRN2", target_bir_lowering=False, num_devices=1)
    arrays = {}

    def dram_in(name, a):
        a = np.ascontiguousarray(a)
        arrays[name] = a
        return nc.dram_tensor(name, a.shape, mybir.dt.from_np(a.dtype), kind="ExternalInput").ap()

    filter_0 = np.asarray(inputs["L0_rec_filter_0"]).reshape(FIELDS, FIELDS, MAPS)
    dense_t = dram_in("dense_t", np.asarray(inputs["dense_ctx"]).T)
    ids = dram_in("ids_in", inputs["ids"])
    tables = [dram_in(f"tbl_{f}", inputs[f"tbl_{f}"]) for f in range(FIELDS)]
    top = [dram_in(n, inputs[n]) for n in ("W_top1", "b_top1", "W_top2", "b_top2", "W_top3")]
    w0_wide = dram_in("w0_wide", np.concatenate([filter_0, filter_0], axis=1))
    w0_tall = dram_in("w0_tall", np.concatenate([filter_0, filter_0], axis=0))
    w1 = dram_in("w1", inputs["L0_rec_filter_1"])
    identity = dram_in("identity", np.eye(P, dtype=np.float32))
    out = nc.dram_tensor("y", (inputs["ids"].shape[0], 1), F32, kind="ExternalOutput").ap()
    build_cin_tower(nc, dense_t, ids, tables, *top, w0_wide, w0_tall, w1, identity, out)
    r = run_bass_kernel_spmd(nc, [arrays], core_ids=[0])
    return r.results[0]["y"]
```

```python
from contextlib import ExitStack

import concourse.bass as bass
from concourse import mybir

F32 = mybir.dt.float32
F32R = mybir.dt.float32r
I32 = mybir.dt.int32
U32 = mybir.dt.uint32
ALU = mybir.AluOpType
ACT = mybir.ActivationFunctionType

P = 128
FIELDS = 32
DIM = 32
MAPS = 128
GROUPS = 4
PER_GROUP = DIM // GROUPS
BLOCKS = PER_GROUP // 2
COLS = BLOCKS * P
PER_TILE = 2 * GROUPS
SHIFTS = 16
ST = 4
FAR = 0
QUAD = 4
QUADS = FIELDS // QUAD
SCALED = 4
SUMMED = QUADS - SCALED
ACT_BANKS = 2
VEC_BANKS = 4
PIECES = 2
W1_PARTS = 4
EARLY = 48
GATHERS = 4
DMA = 16


def build_cin_tower(nc: bass.Bass, dense_t, ids, tables, w_top1, b_top1, w_top2, b_top2, w_top3,
                    w0_wide, w0_tall, w1, identity, picks, out):
    B = ids.shape[0]
    TILES = B // P
    STRIPS = TILES * PER_TILE
    CTX = dense_t.shape[0]
    N1, N2 = w_top1.shape[1], w_top2.shape[1]
    M1, M2 = N1 // P, N2 // P

    x_rows = nc.dram_tensor("x_rows", [STRIPS, 2 * FIELDS, COLS], F32).ap()

    with ExitStack() as ctx:
        def sb(name, shape, dt=F32):
            return ctx.enter_context(nc.sbuf_tensor(name, shape, dt))

        def psum(name, shape):
            return ctx.enter_context(nc.psum_tensor(name, shape, F32))

        def sem(name):
            return ctx.enter_context(nc.semaphore(name))

        ids_sb = sb("ids_sb", [P, TILES, FIELDS], I32)
        emb = sb("emb", [P, TILES * FIELDS * DIM])
        ident = sb("ident", [P, P])
        picks_sb = sb("picks_sb", [P, ST + 2, P])
        xt = sb("xt", [P, 2, COLS])
        w0a, w0b = sb("w0a", [P, ST, MAPS]), sb("w0b", [P, ST, MAPS])
        w0_far_raw = sb("w0_far_raw", [3 * FIELDS, MAPS])
        w0 = sb("w0", [P, ST, MAPS])
        w0_far = sb("w0_far", [3 * FIELDS, MAPS], F32R)
        w1_raw = sb("w1_raw", [P, FIELDS * MAPS])
        w1_hi = sb("w1_hi", [P, FIELDS * MAPS], F32R)
        w1_lo = sb("w1_lo", [P, FIELDS * MAPS], F32R)
        x_shift = sb("x_shift", [P, 2, 1 + ST, COLS])
        x_four = sb("x_four", [P, 2, COLS])
        z = sb("z", [P, 1 + ST, COLS])
        far = sb("far", [3 * FIELDS, COLS], F32R)
        cur0_hi = sb("cur0_hi", [P, 2, COLS], F32R)
        cur0_lo = sb("cur0_lo", [P, 2, COLS], F32R)
        xs = sb("xs", [P, 2, FIELDS, BLOCKS])
        scaled = sb("scaled", [P, 2, SCALED, QUAD, MAPS])
        part = sb("part", [P, 2, QUAD, MAPS])
        chain = sb("chain", [P, 2, QUAD, MAPS])
        fold_sb = sb("fold_sb", [P, 2, MAPS])
        cur1 = sb("cur1", [P, 2, BLOCKS, MAPS])
        acc0 = sb("acc0", [P, TILES, COLS])
        acc1 = sb("acc1", [P, TILES, COLS])
        pooled1_t = sb("pooled1_t", [P, TILES, MAPS])
        pooled = sb("pooled", [P, 2, B])
        ctx_sb = sb("ctx_sb", [CTX, B])
        wt1 = sb("wt1", [P, 2, N1])
        wt1_ctx = sb("wt1_ctx", [CTX, N1])
        wt2 = sb("wt2", [P, M1, N2])
        wt3 = sb("wt3", [P, M2])
        bt1 = sb("bt1", [P, M1])
        bt2 = sb("bt2", [P, M2])
        h1 = sb("h1", [P, M1, B])
        h2 = sb("h2", [P, M2, B])
        y_sb = sb("y_sb", [1, B])

        ps_x = psum("ps_x", [P, COLS])
        ps0 = psum("ps0", [P, COLS])
        act_sums = psum("act_sums", [P, ACT_BANKS, QUAD * MAPS])
        vec_sums = psum("vec_sums", [P, VEC_BANKS, QUAD * MAPS])
        far_whole = z[0:3 * FIELDS, FAR, :]
        first_shift, first_four, first_far = vec_sums, act_sums[:, 0, :], act_sums[:, 1, :]
        ps_h1 = [act_sums[:, 0, 0:B], act_sums[:, 1, 0:B], ps_x[:, 0:B], vec_sums[:, 0, 0:B]]
        ps_h2 = [vec_sums[:, 1, 0:B], vec_sums[:, 2, 0:B]]
        ps_pooled, ps_y = ps0, vec_sums[0:1, 3, 0:B]
        assert (M1, M2, ACT_BANKS, VEC_BANKS) == (len(ps_h1), len(ps_h2), 2, 4)

        ids_in = sem("ids_in")
        ident_in = sem("ident_in")
        picks_in = sem("picks_in")
        w0_in = sem("w0_in")
        w1_in = [sem(f"w1_in{i}") for i in range(W1_PARTS)]
        top_in = sem("top_in")
        gathered = [sem(f"gathered{t}") for t in range(TILES)]
        w0_high = sem("w0_high")
        w1_high = sem("w1_high")
        w0_ready = sem("w0_ready")
        w1_ready = sem("w1_ready")
        cleared = sem("cleared")
        x_turned = sem("x_turned")
        x_copied = sem("x_copied")
        x_stored = [sem(f"x_stored{s}") for s in range(2)]
        picked = sem("picked")
        first_four_ready = sem("first_four_ready")
        shift_in = [sem(f"shift_in{s}") for s in range(2)]
        z_ready = sem("z_ready")
        far_hi_ready = sem("far_hi_ready")
        far_ready = sem("far_ready")
        l0_done = sem("l0_done")
        cur0_hi_ready = sem("cur0_hi_ready")
        cur0_lo_ready = sem("cur0_lo_ready")
        xs_ready = sem("xs_ready")
        act_sums_ready = sem("act_sums_ready")
        vec_sums_ready = sem("vec_sums_ready")
        act_scaled = sem("act_scaled")
        vec_added = sem("vec_added")
        part_added = sem("part_added")
        folded = sem("folded")
        acc0_done = sem("acc0_done")
        acc1_done = sem("acc1_done")
        pooling = sem("pooling")
        pooled0_ready = sem("pooled0_ready")
        pooled1_t_ready = sem("pooled1_t_ready")
        pooled1_turned = sem("pooled1_turned")
        pooled1_ready = sem("pooled1_ready")
        h1_sum, h2_sum, y_sum = sem("h1_sum"), sem("h2_sum"), sem("y_sum")
        h1_ready, h2_ready, y_ready = sem("h1_ready"), sem("h2_ready"), sem("y_ready")
        y_stored = sem("y_stored")

        W0_DMAS = 2 * SHIFTS // ST + 1
        TOP_DMAS = 7
        SHIFT_DMAS = 3
        VEC_UNITS = SUMMED * BLOCKS
        PAIRS = QUAD // 2
        ADDS = SCALED - 1
        PART = FIELDS * MAPS // W1_PARTS
        PRODUCT_PLACES = [(1, 2), (2, 1)]
        FAR_HIGH_PLACE, FAR_LOW_PLACE = (3, 2), (2, 3)
        LAYER1_PLACES = [(2, 2), (3, 0), (3, 2), (3, 3)]
        assert (SCALED * BLOCKS) % ACT_BANKS == 0 and VEC_UNITS % VEC_BANKS == 0
        assert EARLY >= FIELDS and len(PRODUCT_PLACES) == PIECES == 2 and len(LAYER1_PLACES) == ST

        def is_number(a, below):
            return isinstance(a, int) and a < below

        def turned_in(a):
            if isinstance(a, int) and a % PER_TILE >= PER_TILE - 2 and a // PER_TILE + 1 < TILES:
                return 2 * (a // PER_TILE + 1) + a % PER_TILE - (PER_TILE - 2)
            return None

        def turn_bank(half_tile):
            return ps0[:] if half_tile == 1 else ps_x[:]

        def all_steps(eng, step):
            for a in range(1, PER_TILE):
                step(a, a % 2)
            for t in range(1, TILES):
                first = t * PER_TILE // 2
                with eng.Fori(first, first + PER_TILE // 2 - 1) as k:
                    step(2 * k, 0, t)
                    step(2 * k + 1, 1, t)
                step(t * PER_TILE + PER_TILE - 2, 0)
                step(t * PER_TILE + PER_TILE - 1, 1)

        block = ctx.enter_context(nc.Block())

        @block.gpsimd
        def _(pool):
            def gather(n):
                t, f = n // FIELDS, n % FIELDS
                at = n * DIM
                nc.gpsimd.indirect_dma_start(
                    out=emb[:, at:at + DIM], out_offset=None, in_=tables[f],
                    in_offset=bass.IndirectOffsetOnAxis(ap=ids_sb[:, t, f:f + 1].bitcast(U32), axis=0),
                ).then_inc(gathered[t], DMA)

            def add_part(b, sb, n):
                pool.wait_ge(act_scaled, SCALED * b + n + 2)
                if n > 0:
                    pool.wait_ge(part_added, ADDS * b + n)
                elif not is_number(b, 2):
                    pool.wait_ge(vec_added, PAIRS * (SUMMED * (b - 2) + 1))
                nc.gpsimd.tensor_tensor(part[:, sb], scaled[:, sb, 0] if n == 0 else part[:, sb],
                                        scaled[:, sb, n + 1], ALU.add).then_inc(part_added, 1)

            def fold(c, sc, e, n):
                b = BLOCKS * c + e
                sb = e % 2
                if n == 0:
                    pool.wait_ge(vec_added, PAIRS * SUMMED * (b + 1))
                    if not is_number(b, 1):
                        pool.wait_ge(folded, 2 * b)
                    nc.gpsimd.tensor_tensor(fold_sb[:], chain[:, sb, 0:2], chain[:, sb, 2:4],
                                            ALU.add).then_inc(folded, 1)
                else:
                    pool.wait_ge(folded, 2 * b + 1)
                    if e == 0 and not is_number(c, 2):
                        pool.wait_ge(acc1_done, c - 1)
                    nc.gpsimd.tensor_tensor(cur1[:, sc, e], fold_sb[:, 0], fold_sb[:, 1],
                                            ALU.add).then_inc(folded, 1)

            def step(a, s, gathers=()):
                c = a - 1
                for e in range(BLOCKS):
                    if e < len(gathers):
                        gather(gathers[e])
                    ahead = BLOCKS * c + e + 1
                    no_ahead = isinstance(a, int) and a == STRIPS and e == BLOCKS - 1
                    behind = c if e > 0 else c - 1
                    for n in range(ADDS):
                        if not no_ahead:
                            add_part(ahead, (e + 1) % 2, n)
                        if not is_number(behind, 0) and n < 2:
                            fold(behind, 1 - s if e > 0 else s, (e - 1) % BLOCKS, n)

            pool.wait_ge(ids_in, DMA)
            for n in range(EARLY):
                gather(n)
            for n in range(ADDS):
                add_part(0, 0, n)
            done = EARLY
            total = TILES * FIELDS
            looped = 2 * -(-(1 + -(-(total - EARLY) // GATHERS)) // 2)
            for a in range(1, looped):
                step(a, a % 2, range(done, min(done + GATHERS, total)))
                done += GATHERS
            with pool.Fori(looped // 2, STRIPS // 2) as k:
                step(2 * k, 0)
                step(2 * k + 1, 1)
            step(STRIPS, 0)

        @block.sync
        def _(sp):
            def store_x(half_tile):
                t, half = half_tile // 2, half_tile % 2
                sp.wait_ge(x_copied, half_tile + 1)
                strips = x_rows[t * PER_TILE:(t + 1) * PER_TILE].rearrange(
                    "(g two) f c -> two g f c", two=2)[half]
                for twice in range(2):
                    sp.dma_start(strips[:, twice * FIELDS:(twice + 1) * FIELDS, :].rearrange("g f c -> f g c"),
                                 xt[:, half, :]).then_inc(x_stored[half], DMA)

            def load_shift(a, t, s):
                sp.wait_ge(x_stored[s], (t + 1) * 2 * DMA)
                first = x_rows[bass.ds(a, 1), 0:1, :].rearrange("o f c -> (o f) c")
                sp.dma_start(x_four[:, s], bass.AP(first.tensor, first.offset,
                                                   [[0, SHIFTS // ST], [COLS, FIELDS], [1, COLS]]),
                             ).then_inc(shift_in[s], DMA)
                sp.dma_start(x_shift[:, s, FAR], bass.AP(first.tensor, first.offset + SHIFTS * COLS,
                                                         [[0, SHIFTS // ST], [COLS, FIELDS], [1, COLS]]),
                             ).then_inc(shift_in[s], DMA)
                sp.dma_start(x_shift[:, s, 1:].rearrange("p t c -> p (t c)"),
                             bass.AP(first.tensor, first.offset,
                                     [[ST * COLS, SHIFTS // ST], [COLS, FIELDS], [1, ST * COLS]]),
                             ).then_inc(shift_in[s], DMA)

            def step(a, s, tile=None):
                turn = turned_in(a)
                if turn is not None:
                    store_x(turn)
                if isinstance(a, int) and a == STRIPS - 1:
                    return
                sp.wait_ge(z_ready, PIECES * a)
                load_shift(a + 1, (a + 1) // PER_TILE if isinstance(a, int) else tile, 1 - s)

            sp.dma_start(ids_sb[:], ids.rearrange("(t p) f -> p t f", p=P)).then_inc(ids_in, DMA)
            sp.dma_start(ident[:], identity).then_inc(ident_in, DMA)
            sp.dma_start(picks_sb[:], picks).then_inc(picks_in, DMA)
            for sq in range(SHIFTS // ST):
                for a, src, step_h, step_s in ((w0a, w0_wide, 2 * FIELDS + 1, 1),
                                               (w0b, w0_tall, FIELDS + 1, FIELDS)):
                    sp.dma_start(
                        a[sq * FIELDS:(sq + 1) * FIELDS],
                        bass.AP(src.tensor, ST * sq * step_s * MAPS,
                                [[step_h * MAPS, FIELDS], [step_s * MAPS, ST], [1, MAPS]]),
                    ).then_inc(w0_in, DMA)
            sp.dma_start(w0_far_raw[:], bass.AP(w0_wide.tensor, SHIFTS * MAPS,
                                                [[0, 3], [(2 * FIELDS + 1) * MAPS, FIELDS], [1, MAPS]]),
                         ).then_inc(w0_in, DMA)
            w1_v = w1.rearrange("o (h m) n -> (o m) h n", m=MAPS)
            per = FIELDS // W1_PARTS
            for i in range(W1_PARTS):
                sp.dma_start(w1_raw[:, i * PART:(i + 1) * PART].rearrange("p (h n) -> p h n", n=MAPS),
                             w1_v[:, i * per:(i + 1) * per, :]).then_inc(w1_in[i], DMA)
            store_x(1)
            load_shift(1, 0, 1)
            store_x(0)
            sp.dma_start(ctx_sb[:], dense_t).then_inc(top_in, DMA)
            sp.dma_start(wt1[:], w_top1[0:2 * P].rearrange("(k p) n -> p k n", p=P)).then_inc(top_in, DMA)
            sp.dma_start(wt1_ctx[:], w_top1[2 * P:2 * P + CTX]).then_inc(top_in, DMA)
            sp.dma_start(wt2[:], w_top2.rearrange("(k p) n -> p k n", p=P)).then_inc(top_in, DMA)
            with nc.allow_non_contiguous_dma(reason="a few hundred bias and column words"):
                sp.dma_start(wt3[:], w_top3.rearrange("(k p) o -> p (k o)", p=P)).then_inc(top_in, DMA)
                sp.dma_start(bt1[:], b_top1.rearrange("(k p) -> p k", p=P)).then_inc(top_in, DMA)
                sp.dma_start(bt2[:], b_top2.rearrange("(k p) -> p k", p=P)).then_inc(top_in, DMA)
            all_steps(sp, step)
            sp.wait_ge(y_ready, 1)
            sp.dma_start(out.rearrange("b o -> o b"), y_sb[:]).then_inc(y_stored, DMA)
            sp.wait_ge(y_stored, DMA)

        @block.scalar
        def _(act):
            def copy_x(half_tile):
                act.wait_ge(x_turned, half_tile + 1)
                t, half = half_tile // 2, half_tile % 2
                if t > 0:
                    act.wait_ge(x_stored[half], t * 2 * DMA)
                nc.scalar.copy(xt[:, half, :], turn_bank(half_tile)).then_inc(x_copied, 1)

            def take_cur0(a, s):
                act.wait_ge(l0_done, a + 1)
                nc.scalar.activation(cur0_hi[:, s, :], ps0[:], ACT.Relu).then_inc(cur0_hi_ready, 1)

            def take_xs(a, s, tile):
                if not is_number(a, 2):
                    act.wait_ge(vec_added, PAIRS * VEC_UNITS * (a - 1))
                    act.wait_ge(act_scaled, SCALED * BLOCKS * (a - 1))
                if isinstance(a, int):
                    at = FIELDS * DIM * (a // PER_TILE) + BLOCKS * (a % PER_TILE)
                    rows = emb[:, at:at + (FIELDS - 1) * DIM + BLOCKS]
                    act.wait_ge(gathered[a // PER_TILE], FIELDS * DMA)
                else:
                    at = tile * FIELDS * DIM + (a - tile * PER_TILE) * BLOCKS
                    rows = emb[:, bass.ds(at, (FIELDS - 1) * DIM + BLOCKS)]
                first = rows[:, 0:1]
                nc.scalar.copy(xs[:, s], bass.AP(first.tensor, first.offset,
                                                 [first.ap[0], [DIM, FIELDS], [1, BLOCKS]])
                               ).then_inc(xs_ready, 1)

            def scale_quad(b, sc, e, n):
                bank = (SCALED * e + n) % ACT_BANKS
                act.wait_ge(act_sums_ready, SCALED * b + n + 1)
                if not is_number(b, 2):
                    act.wait_ge(part_added, ADDS * (b - 1))
                for i in range(QUAD):
                    last = nc.scalar.activation(scaled[:, e % 2, n, i, :],
                                                act_sums[:, bank, i * MAPS:(i + 1) * MAPS], ACT.Copy,
                                                scale=xs[:, sc, QUAD * n + i, e:e + 1])
                last.then_inc(act_scaled, 1)

            def far_high(a):
                if not is_number(a, 1):
                    act.wait_ge(l0_done, a)
                act.wait_ge(z_ready, PIECES * a + (PIECES if is_number(a, 2) else 1))
                nc.scalar.copy(far[:], far_whole).then_inc(far_hi_ready, 1)

            def step(a, s, tile=None):
                c = a - 1
                last = isinstance(a, int) and a == STRIPS
                turn = turned_in(a)
                if turn is not None:
                    copy_x(turn)
                if not last:
                    take_cur0(a, s)
                for e in range(1, BLOCKS):
                    for n in range(SCALED):
                        scale_quad(BLOCKS * c + e, 1 - s, e, n)
                        if (e, n) == FAR_HIGH_PLACE and not (isinstance(a, int) and a >= STRIPS - 1):
                            far_high(a + 1)
                    if e == 1 and not last:
                        take_xs(a, s, tile)
                if not last:
                    act.wait_ge(xs_ready, a + 1)
                    for n in range(SCALED):
                        scale_quad(BLOCKS * a, s, 0, n)

            act.wait_ge(w0_in, W0_DMAS * DMA)
            nc.scalar.copy(w0_far[:], w0_far_raw[:]).then_inc(w0_high, 1)
            for i in range(W1_PARTS):
                cols = slice(i * PART, (i + 1) * PART)
                act.wait_ge(w1_in[i], DMA)
                nc.scalar.copy(w1_hi[:, cols], w1_raw[:, cols]).then_inc(w1_high, 1)
            copy_x(0)
            copy_x(1)
            act.wait_ge(picked, 1)
            nc.scalar.copy(x_four[:, 0], first_four).then_inc(first_four_ready, 1)
            take_xs(0, 0, 0)
            far_high(0)
            take_cur0(0, 0)
            act.wait_ge(xs_ready, 1)
            for n in range(SCALED):
                scale_quad(0, 0, 0, n)
                if n == 1:
                    far_high(1)
            all_steps(act, step)
            step(STRIPS, 0)
            act.wait_ge(pooled1_turned, TILES)
            nc.scalar.copy(pooled[:, 1, :], ps_pooled[:, 0:B]).then_inc(pooled1_ready, 1)
            act.wait_ge(top_in, TOP_DMAS * DMA)
            for m in range(M1):
                act.wait_ge(h1_sum, m + 1)
                nc.scalar.activation(h1[:, m, :], ps_h1[m], ACT.Relu,
                                     bias=bt1[:, m:m + 1]).then_inc(h1_ready, 1)
            for m in range(M2):
                act.wait_ge(h2_sum, m + 1)
                nc.scalar.activation(h2[:, m, :], ps_h2[m], ACT.Relu,
                                     bias=bt2[:, m:m + 1]).then_inc(h2_ready, 1)
            act.wait_ge(y_sum, 1)
            nc.scalar.copy(y_sb[:], ps_y).then_inc(y_ready, 1)

        @block.vector
        def _(dve):
            def wait_factors(a, s, filling):
                dve.wait_ge(shift_in[s], (filling + s) * SHIFT_DMAS * DMA)

            def layer1_product(a, s, piece):
                tiles = slice(1 + ST // 2 if piece else 0, 1 + ST if piece else 1 + ST // 2)
                if piece == 0:
                    dve.wait_ge(l0_done, a)
                    dve.wait_ge(far_ready, a)
                multiply(tiles, x_shift[:, s, tiles], s).then_inc(z_ready, 1)

            def multiply(tiles, shift, s):
                copies = tiles.stop - tiles.start
                return nc.vector.tensor_tensor(z[:, tiles], shift,
                                               x_four[:, s].unsqueeze(1).to_broadcast([P, copies, COLS]),
                                               ALU.mult)

            def early_products(a, shift, far_factor):
                if a == 0:
                    dve.wait_ge(first_four_ready, 1)
                    dve.wait_ge(picked, 1 + ST // 2)
                else:
                    dve.wait_ge(l0_done, a)
                multiply(slice(1, 1 + ST // 2), shift[:, 0:ST // 2], a).then_inc(z_ready, 1)
                if a == 0:
                    dve.wait_ge(picked, 2 + ST // 2)
                multiply(slice(FAR, FAR + 1), far_factor, a)
                if a == 0:
                    dve.wait_ge(picked, 2 + ST)
                multiply(slice(1 + ST // 2, 1 + ST), shift[:, ST // 2:ST], a).then_inc(z_ready, 1)

            def far_low(a):
                dve.wait_ge(far_hi_ready, a + 1)
                low = slice(2 * FIELDS, 3 * FIELDS)
                nc.vector.tensor_tensor(far[low], z[low, FAR, :], far[low],
                                        ALU.subtract).then_inc(far_ready, 1)

            def take_cur0(a, s):
                dve.wait_ge(cur0_hi_ready, a + 1)
                nc.vector.scalar_tensor_tensor(out=cur0_lo[:, s, :], in0=ps0[:], scalar=0.0,
                                               in1=cur0_hi[:, s, :].bitcast(F32), op0=ALU.max,
                                               op1=ALU.subtract).then_inc(cur0_lo_ready, 1)

            def tile_of(acc, a):
                if isinstance(a, int):
                    return acc[:, a // PER_TILE, :]
                at = (a & (STRIPS - PER_TILE)) * (COLS // PER_TILE)
                return acc[:].rearrange("p t c -> p (t c)")[:, bass.ds(at, COLS)]

            def add(acc, done, a, sums):
                if not is_number(a, 1):
                    dve.wait_ge(done, a)
                into = tile_of(acc, a)
                nc.vector.scalar_tensor_tensor(out=into, in0=sums, scalar=0.0, in1=into, op0=ALU.max,
                                               op1=ALU.add).then_inc(done, 1)

            def add1(c, s):
                dve.wait_ge(folded, 2 * BLOCKS * (c + 1))
                add(acc1, acc1_done, c, cur1[:, s].rearrange("p e n -> p (e n)"))

            def add_quad(c, sc, e, n):
                b = BLOCKS * c + e
                unit = VEC_UNITS * c + SUMMED * e + n
                sb = e % 2
                bank = (SUMMED * e + n) % VEC_BANKS
                dve.wait_ge(vec_sums_ready, unit + 1)
                if n == 0:
                    dve.wait_ge(part_added, ADDS * (b + 1))
                    if not is_number(b, 2):
                        dve.wait_ge(folded, 2 * (b - 2) + 1)
                for i in range(QUAD):
                    if n > 0 and i % 2 == 0:
                        dve.wait_ge(vec_added, PAIRS * (unit - 1) + i // 2 + 1)
                    last = nc.vector.scalar_tensor_tensor(
                        out=chain[:, sb, i, :], in0=vec_sums[:, bank, i * MAPS:(i + 1) * MAPS],
                        scalar=xs[:, sc, QUAD * (SCALED + n) + i, e:e + 1],
                        in1=part[:, sb, i, :] if n == 0 else chain[:, sb, i, :],
                        op0=ALU.mult, op1=ALU.add)
                    if i % 2 == 1:
                        last.then_inc(vec_added, 1)

            def step(a, s, tile=None):
                c = a - 1
                last = isinstance(a, int) and a == STRIPS
                half_a = a // 2 if isinstance(a, int) else (a - s) // 2
                dve.wait_ge(xs_ready, a)
                for e in range(BLOCKS):
                    for n in range(SUMMED):
                        add_quad(c, 1 - s, e, n)
                        if e == 0 and n == 1 and not last:
                            take_cur0(a, s)
                        if e == 0 and n == 2 and not last:
                            add(acc0, acc0_done, a, ps0[:])
                        if (e, n) == (3, 1) and not is_number(a, 2):
                            add1(a - 2, s)
                        if isinstance(a, int) and a == STRIPS - 1 and (e, n) == (1, 2):
                            pool_dims(acc0, acc0_done, slice(0, TILES), pooled0, pooled0_ready)
                        if isinstance(a, int) and a == STRIPS - 1 and (e, n) == (2, 2):
                            pool_dims(acc1, acc1_done, slice(0, TILES - 1), pooled1_t[:, 0:TILES - 1],
                                      pooled1_t_ready)
                        if isinstance(a, int) and a >= STRIPS - 1:
                            continue
                        if (e, n) == PRODUCT_PLACES[0]:
                            wait_factors(a + 1, 1 - s, half_a + s)
                        if (e, n) in PRODUCT_PLACES:
                            layer1_product(a + 1, 1 - s, PRODUCT_PLACES.index((e, n)))
                        if (e, n) == FAR_LOW_PLACE:
                            far_low(a + 1)

            def pool_dims(acc, done, tiles, into, ready):
                dve.wait_ge(done, PER_TILE * tiles.stop)
                nc.vector.tensor_tensor(acc[:, tiles, 0:2 * P], acc[:, tiles, 0:2 * P],
                                        acc[:, tiles, 2 * P:4 * P], ALU.add).then_inc(pooling, 1)
                pool_dims.steps += 1
                dve.wait_ge(pooling, pool_dims.steps)
                nc.vector.tensor_tensor(into, acc[:, tiles, 0:P], acc[:, tiles, P:2 * P],
                                        ALU.add).then_inc(ready, 1)

            pool_dims.steps = 0
            pooled0 = pooled[:, 0, :].rearrange("p (t b) -> p t b", t=TILES)
            nc.vector.memset(acc0[:], 0.0).then_inc(cleared, 1)
            nc.vector.memset(acc1[:], 0.0).then_inc(cleared, 1)
            dve.wait_ge(w0_in, W0_DMAS * DMA)
            nc.vector.memset(w0b[0:FIELDS, 0, :], 0.0).then_inc(w0_ready, 1)
            dve.wait_ge(w0_ready, 1)
            nc.vector.tensor_tensor(w0[:], w0a[:], w0b[:], ALU.add).then_inc(w0_ready, 1)
            dve.wait_ge(w0_high, 1)
            low = slice(FIELDS, 2 * FIELDS)
            nc.vector.tensor_tensor(w0_far[low], w0_far_raw[low], w0_far[low],
                                    ALU.subtract).then_inc(w0_ready, 1)
            for i in range(W1_PARTS):
                cols = slice(i * PART, (i + 1) * PART)
                dve.wait_ge(w1_high, i + 1)
                nc.vector.tensor_tensor(w1_lo[:, cols], w1_raw[:, cols], w1_hi[:, cols],
                                        ALU.subtract).then_inc(w1_ready, 1)
            dve.wait_ge(cleared, 2)
            early_products(0, first_shift, first_far.unsqueeze(1))
            far_low(0)
            take_cur0(0, 0)
            add(acc0, acc0_done, 0, ps0[:])
            wait_factors(1, 1, 0)
            early_products(1, x_shift[:, 1, 1:], x_shift[:, 1, FAR:FAR + 1])
            far_low(1)
            all_steps(dve, step)
            step(STRIPS, 0)
            sb, e = (BLOCKS - 1) % 2, BLOCKS - 1
            dve.wait_ge(vec_added, PAIRS * VEC_UNITS * STRIPS)
            dve.wait_ge(folded, 2 * (BLOCKS * STRIPS - 1))
            nc.vector.tensor_tensor(fold_sb[:], chain[:, sb, 0:2], chain[:, sb, 2:4],
                                    ALU.add).then_inc(folded, 1)
            dve.wait_ge(folded, 2 * (BLOCKS * STRIPS - 1) + 1)
            nc.vector.tensor_tensor(cur1[:, 1, e], fold_sb[:, 0], fold_sb[:, 1],
                                    ALU.add).then_inc(folded, 1)
            add1(STRIPS - 1, 1)
            pool_dims(acc1, acc1_done, slice(TILES - 1, TILES), pooled1_t[:, TILES - 1:TILES],
                      pooled1_t_ready)

        @block.tensor
        def _(pe):
            def turn_x(half_tile):
                t, half = half_tile // 2, half_tile % 2
                pe.wait_ge(gathered[t], FIELDS * DMA)
                src = emb[:, t * FIELDS * DIM:(t + 1) * FIELDS * DIM].rearrange(
                    "p (fg e) -> p e fg", e=PER_GROUP)
                if half_tile > 1:
                    pe.wait_ge(x_copied, half_tile)
                for e in range(BLOCKS):
                    last = nc.tensor.transpose(turn_bank(half_tile)[:, e * P:(e + 1) * P], src[:, half * BLOCKS + e],
                                               ident[:])
                last.then_inc(x_turned, 1)

            def layer1(a, t):
                pe.wait_ge(z_ready, PIECES * a + t * PIECES // ST + 1)
                if t == 0 and not is_number(a, 1):
                    pe.wait_ge(acc0_done, a)
                nc.tensor.matmul(ps0[:], w0[:, t, :], z[:, 1 + t, :], start=(t == 0), stop=False)

            def layer1_far(a):
                pe.wait_ge(far_ready, a + 1)
                nc.tensor.matmul(ps0[:], w0_far[:], far[:], start=False, stop=True).then_inc(l0_done, 1)

            def quad(bank, sc, e, q):
                cols, maps = slice(e * P, (e + 1) * P), slice(q * QUAD * MAPS, (q + 1) * QUAD * MAPS)
                hi, lo = cur0_hi[:, sc, cols], cur0_lo[:, sc, cols]
                nc.tensor.matmul(bank, hi, w1_lo[:, maps], start=True, stop=False)
                nc.tensor.matmul(bank, hi, w1_hi[:, maps], start=False, stop=False)
                return nc.tensor.matmul(bank, lo, w1_hi[:, maps], start=False, stop=True)

            def quad_for_act(b, sc, e, n):
                unit = SCALED * b + n
                if not is_number(unit, ACT_BANKS):
                    pe.wait_ge(act_scaled, unit - ACT_BANKS + 1)
                quad(act_sums[:, (SCALED * e + n) % ACT_BANKS, :], sc, e, n).then_inc(act_sums_ready, 1)

            def quad_for_vec(c, sc, e, n):
                unit = VEC_UNITS * c + SUMMED * e + n
                if not is_number(unit, VEC_BANKS):
                    pe.wait_ge(vec_added, PAIRS * (unit - VEC_BANKS + 1))
                quad(vec_sums[:, (SUMMED * e + n) % VEC_BANKS, :], sc, e,
                     SCALED + n).then_inc(vec_sums_ready, 1)

            def top_early(m):
                cols = slice(m * P, (m + 1) * P)
                if m == 0:
                    pe.wait_ge(top_in, TOP_DMAS * DMA)
                    pe.wait_ge(pooled0_ready, 1)
                if m < ACT_BANKS:
                    pe.wait_ge(act_scaled, SCALED * BLOCKS * STRIPS - ACT_BANKS + m + 1)
                nc.tensor.matmul(ps_h1[m], wt1_ctx[:, cols], ctx_sb[:], start=True, stop=False)
                nc.tensor.matmul(ps_h1[m], wt1[:, 0, cols], pooled[:, 0, :], start=False, stop=False)

            def step(a, s, tile=None):
                c = a - 1
                last = isinstance(a, int) and a == STRIPS
                turn = turned_in(a)
                if turn is not None:
                    turn_x(turn)
                if not last:
                    layer1_far(a)
                for e in range(BLOCKS):
                    if e == BLOCKS - 1 and not last:
                        pe.wait_ge(cur0_lo_ready, a + 1)
                    for n in range(max(SCALED, SUMMED)):
                        if n < SUMMED:
                            quad_for_vec(c, 1 - s, e, n)
                        if n < SCALED and e < BLOCKS - 1:
                            quad_for_act(BLOCKS * c + e + 1, 1 - s, e + 1, n)
                        elif n < SCALED and not last:
                            quad_for_act(BLOCKS * a, s, 0, n)
                        if (e, n) in LAYER1_PLACES and not (isinstance(a, int) and a >= STRIPS - 1):
                            layer1(a + 1, LAYER1_PLACES.index((e, n)))

            pe.wait_ge(ident_in, DMA)
            turn_x(0)
            turn_x(1)
            pe.wait_ge(picks_in, DMA)
            pe.wait_ge(x_copied, 1)
            order = [(first_shift[:, t, :], t) for t in range(ST)]
            order.insert(ST // 2, (first_far, ST + 1))
            for bank, k in [(first_four, ST)] + order:
                nc.tensor.matmul(bank, picks_sb[:, k, :], xt[:, 0, :], start=True,
                                 stop=True).then_inc(picked, 1)
            pe.wait_ge(x_copied, 2)
            pe.wait_ge(w0_ready, 3)
            for t in range(ST):
                layer1(0, t)
            layer1_far(0)
            pe.wait_ge(w1_ready, W1_PARTS)
            pe.wait_ge(cur0_lo_ready, 1)
            for n in range(SCALED):
                quad_for_act(0, 0, 0, n)
                layer1(1, n)
            all_steps(pe, step)
            step(STRIPS, 0)

            for m in range(M1 - 1):
                top_early(m)
            pe.wait_ge(vec_added, PAIRS * (VEC_UNITS * STRIPS - VEC_BANKS + 1))
            top_early(M1 - 1)
            for t in range(TILES):
                pe.wait_ge(pooled1_t_ready, 2 if t == TILES - 1 else 1)
                nc.tensor.transpose(ps_pooled[:, t * P:(t + 1) * P], pooled1_t[:, t, :],
                                    ident[:]).then_inc(pooled1_turned, 1)
            pe.wait_ge(pooled1_ready, 1)
            for m in range(M1):
                nc.tensor.matmul(ps_h1[m], wt1[:, 1, m * P:(m + 1) * P], pooled[:, 1, :],
                                 start=False, stop=True).then_inc(h1_sum, 1)
            for k in range(M1):
                pe.wait_ge(h1_ready, k + 1)
                for m in range(M2):
                    one = nc.tensor.matmul(ps_h2[m], wt2[:, k, m * P:(m + 1) * P], h1[:, k, :],
                                           start=(k == 0), stop=(k == M1 - 1))
                    if k == M1 - 1:
                        one.then_inc(h2_sum, 1)
            for k in range(M2):
                pe.wait_ge(h2_ready, k + 1)
                last = nc.tensor.matmul(ps_y, wt3[:, k:k + 1], h2[:, k, :],
                                        start=(k == 0), stop=(k == M2 - 1))
            last.then_inc(y_sum, 1)


def kernel(**inputs):
    import numpy as np
    import concourse.bacc as bacc
    from concourse.bass_utils import run_bass_kernel_spmd

    nc = bacc.Bacc("TRN2", target_bir_lowering=False, num_devices=1)
    arrays = {}

    def dram_in(name, a):
        a = np.ascontiguousarray(a)
        arrays[name] = a
        return nc.dram_tensor(name, a.shape, mybir.dt.from_np(a.dtype), kind="ExternalInput").ap()

    filter_0 = np.asarray(inputs["L0_rec_filter_0"]).reshape(FIELDS, FIELDS, MAPS)
    dense_t = dram_in("dense_t", np.asarray(inputs["dense_ctx"]).T)
    ids = dram_in("ids_in", inputs["ids"])
    tables = [dram_in(f"tbl_{f}", inputs[f"tbl_{f}"]) for f in range(FIELDS)]
    top = [dram_in(n, inputs[n]) for n in ("W_top1", "b_top1", "W_top2", "b_top2", "W_top3")]
    w0_wide = dram_in("w0_wide", np.concatenate([filter_0, filter_0], axis=1))
    w0_tall = dram_in("w0_tall", np.concatenate([filter_0, filter_0], axis=0))
    w1 = dram_in("w1", inputs["L0_rec_filter_1"])
    identity = dram_in("identity", np.eye(P, dtype=np.float32))
    picks = np.zeros((P, ST + 2, P), dtype=np.float32)
    for q in range(SHIFTS // ST):
        for h in range(FIELDS):
            for k, f in enumerate([h + ST * q + t for t in range(ST)] + [h, h + SHIFTS]):
                picks[GROUPS * (f % FIELDS), k, FIELDS * q + h] = 1
    picks = dram_in("picks", picks)
    out = nc.dram_tensor("y", (inputs["ids"].shape[0], 1), F32, kind="ExternalOutput").ap()
    build_cin_tower(nc, dense_t, ids, tables, *top, w0_wide, w0_tall, w1, identity, picks, out)
    r = run_bass_kernel_spmd(nc, [arrays], core_ids=[0])
    return r.results[0]["y"]
```
